# Optimizing a Trainium2 kernel written in Bass

```python
import numpy as np
import jax
import jax.numpy as jnp

def _softmax(x, axis=-1):
    return jax.nn.softmax(x, axis=axis)

def _gelu(x):
    return jax.nn.gelu(x, approximate=True)

def _silu(x):
    return jax.nn.silu(x)

def _sigmoid(x):
    return jax.nn.sigmoid(x)

def _layernorm(x, axis=-1, eps=1e-05):
    m = jnp.mean(x, axis=axis, keepdims=True)
    v = jnp.var(x, axis=axis, keepdims=True)
    return (x - m) / jnp.sqrt(v + eps)

def _scatter_add(tgt, idx, src, axis=0):
    return tgt.at[idx].add(src)

def _segment_sum(src, seg, n):
    return jax.ops.segment_sum(src, seg, n)
kernel_name = 'mk_flamingo_gated_d2_seqx_r4_0b2a6f'

def setup_inputs(seed: int=0):
    np.random.seed(seed)
    _w = jnp.asarray

    def _rec_inputs():
        import jax
        import jax.numpy as jnp
        _rk = jax.random.key(seed)
        x = -0.0002928 + 1 * jax.random.normal(jax.random.fold_in(_rk, 1), (64, 256, 256), jnp.float32)
        _lenS = 256 - jax.random.randint(jax.random.fold_in(_rk, 7), (64,), 0, max(1, 256 // 4) + 1, jnp.int32)
        _lenS2 = 77 - jax.random.randint(jax.random.fold_in(_rk, 8), (64,), 0, max(1, 77 // 4) + 1, jnp.int32)
        _ctx_1024P = jax.random.normal(jax.random.fold_in(_rk, 11), (64, 16, 256), jnp.float32)
        _ctx_1024c = jax.random.dirichlet(jax.random.fold_in(_rk, 511), 0.3 * jnp.ones((16,), jnp.float32), (64, 77))
        _ctx_1024t = jnp.einsum('bsk,bkd->bsd', _ctx_1024c, _ctx_1024P)
        _ctx_1024t = _ctx_1024t * jax.lax.rsqrt(jnp.mean(jnp.square(_ctx_1024t)) + 1e-12) * 0.953939
        ctx_1024 = -1.39393e-06 + 0.999914 * (_ctx_1024t + 0.3 * jax.random.normal(jax.random.fold_in(_rk, 611), (64, 77, 256), jnp.float32))
        _g = jax.random.normal(jax.random.fold_in(_rk, 9001), (2, 2), jnp.float32)
        _g = jnp.sign(_g) * jnp.maximum(jnp.abs(_g), 1.0) + (_g == 0) * 1.0
        g_xattn = _g[0]
        g_ffn = _g[1]
        return (x, ctx_1024, g_xattn, g_ffn)
    x, ctx_1024, g_xattn, g_ffn = _rec_inputs()

    def _L0_xattn_setup():
        import jax, jax.numpy as jnp
        import numpy as np
        D_MODEL = 256
        N_HEAD = 16

        def _split_heads(x):
            B, S, D = x.shape
            return x.reshape(B, S, N_HEAD, D // N_HEAD).transpose(0, 2, 1, 3)
        key = jax.random.key(seed)
        ks = jax.random.split(key, 11)
        B, S, D = (2, 512, D_MODEL)
        s = 1.0 / np.sqrt(D)
        inp = {'q': jax.random.normal(ks[0], (B, S, D), jnp.float32), 'k': jax.random.normal(ks[1], (B, S, D), jnp.float32), 'v': jax.random.normal(ks[2], (B, S, D), jnp.float32), 'w_q': jax.random.normal(ks[3], (D, D), jnp.float32) * s, 'b_q': jnp.zeros((D,), jnp.float32), 'w_k': jax.random.normal(ks[4], (D, D), jnp.float32) * s, 'b_k': jnp.zeros((D,), jnp.float32), 'w_v': jax.random.normal(ks[5], (D, D), jnp.float32) * s, 'b_v': jnp.zeros((D,), jnp.float32), 'w_o': jax.random.normal(ks[6], (D, D), jnp.float32) * s, 'b_o': jnp.zeros((D,), jnp.float32)}
        return inp
    _L0_xattn_all = _L0_xattn_setup()
    _L0_xattn_in = {k: v for k, v in _L0_xattn_all.items() if k in ('w_q', 'b_q', 'w_k', 'b_k', 'w_v', 'b_v', 'w_o', 'b_o')}
    del _L0_xattn_all

    def _L0_ffn_setup():
        import jax, jax.numpy as jnp
        import numpy as np
        SL, BS, HS, FF, E, TOPK = (512, 2, 256, 1024, 8, 2)
        key = jax.random.key(seed)
        ks = jax.random.split(key, 6)
        T = SL * BS
        x = jax.random.normal(ks[0], (SL, BS, HS), jnp.float32)
        scores = jax.random.uniform(ks[1], (T, E), jnp.float32)
        expert_weights = jax.random.uniform(ks[2], (T, TOPK), jnp.float32)
        expert_indices = jax.random.randint(ks[3], (T, TOPK), 0, E, jnp.int32)
        w1 = jax.random.normal(ks[4], (E, HS, FF), jnp.float32) * (1.0 / np.sqrt(HS))
        w2 = jax.random.normal(ks[5], (E, FF, HS), jnp.float32) * (1.0 / np.sqrt(FF))
        bias = jnp.zeros((HS,), jnp.float32)
        return dict(x=x, scores=scores, expert_weights=expert_weights, expert_indices=expert_indices, w1=w1, w2=w2, bias=bias)
    _L0_ffn_all = _L0_ffn_setup()
    _L0_ffn_in = {k: v for k, v in _L0_ffn_all.items() if k in ('scores', 'expert_weights', 'expert_indices', 'w1', 'w2', 'bias')}
    del _L0_ffn_all

    def _L1_xattn_setup():
        import jax, jax.numpy as jnp
        import numpy as np
        key = jax.random.key(seed)
        ks = jax.random.split(key, 7)
        B, S, D, H, Dh = (4, 512, 256, 16, 64)
        return {'query_input': jax.random.normal(ks[0], (B, S, D), jnp.float32), 'key_input': jax.random.normal(ks[1], (B, S, D), jnp.float32), 'value_input': jax.random.normal(ks[2], (B, S, D), jnp.float32), 'Wq': jax.random.normal(ks[3], (D, H, Dh), jnp.float32) * 0.03, 'Wk': jax.random.normal(ks[4], (D, H, Dh), jnp.float32) * 0.03, 'Wv': jax.random.normal(ks[5], (D, H, Dh), jnp.float32) * 0.03, 'Wo': jax.random.normal(ks[6], (H, Dh, D), jnp.float32) * 0.03}
    _L1_xattn_all = _L1_xattn_setup()
    _L1_xattn_in = {k: v for k, v in _L1_xattn_all.items() if k in ('Wq', 'Wk', 'Wv', 'Wo')}
    del _L1_xattn_all

    def _L1_ffn_setup():
        import jax, jax.numpy as jnp
        import numpy as np
        IN_DIM, OUT_DIM, N_PROTO, RANK = (256, 256, 32, 16)
        key = jax.random.key(seed)
        ks = jax.random.split(key, 5)
        x = jax.random.normal(ks[0], (2, 1024, IN_DIM), dtype=jnp.float32)
        prototypes = jax.random.normal(ks[1], (N_PROTO, IN_DIM), dtype=jnp.float32) * 0.02
        B = jax.random.normal(ks[2], (N_PROTO, RANK, IN_DIM), dtype=jnp.float32) * 0.02
        A = jax.random.normal(ks[3], (N_PROTO, OUT_DIM, RANK), dtype=jnp.float32) * 0.02
        bias = jnp.zeros((N_PROTO, OUT_DIM), dtype=jnp.float32)
        temp = jnp.asarray(1.0, dtype=jnp.float32)
        return {'x': x, 'prototypes': prototypes, 'B': B, 'A': A, 'bias': bias, 'temp': temp}
    _L1_ffn_all = _L1_ffn_setup()
    _L1_ffn_in = {k: v for k, v in _L1_ffn_all.items() if k in ('prototypes', 'B', 'A', 'bias', 'temp')}
    del _L1_ffn_all
    return {'x': x, 'ctx_1024': ctx_1024, 'g_xattn': g_xattn, 'g_ffn': g_ffn, 'L0_xattn_w_q': _L0_xattn_in['w_q'], 'L0_xattn_b_q': _L0_xattn_in['b_q'], 'L0_xattn_w_k': _L0_xattn_in['w_k'], 'L0_xattn_b_k': _L0_xattn_in['b_k'], 'L0_xattn_w_v': _L0_xattn_in['w_v'], 'L0_xattn_b_v': _L0_xattn_in['b_v'], 'L0_xattn_w_o': _L0_xattn_in['w_o'], 'L0_xattn_b_o': _L0_xattn_in['b_o'], 'L0_ffn_scores': _L0_ffn_in['scores'], 'L0_ffn_expert_weights': _L0_ffn_in['expert_weights'], 'L0_ffn_expert_indices': _L0_ffn_in['expert_indices'], 'L0_ffn_w1': _L0_ffn_in['w1'], 'L0_ffn_w2': _L0_ffn_in['w2'], 'L0_ffn_bias': _L0_ffn_in['bias'], 'L1_xattn_Wq': _L1_xattn_in['Wq'], 'L1_xattn_Wk': _L1_xattn_in['Wk'], 'L1_xattn_Wv': _L1_xattn_in['Wv'], 'L1_xattn_Wo': _L1_xattn_in['Wo'], 'L1_ffn_prototypes': _L1_ffn_in['prototypes'], 'L1_ffn_B': _L1_ffn_in['B'], 'L1_ffn_A': _L1_ffn_in['A'], 'L1_ffn_bias': _L1_ffn_in['bias'], 'L1_ffn_temp': _L1_ffn_in['temp']}

def reference(x, ctx_1024, g_xattn, g_ffn, L0_xattn_w_q, L0_xattn_b_q, L0_xattn_w_k, L0_xattn_b_k, L0_xattn_w_v, L0_xattn_b_v, L0_xattn_w_o, L0_xattn_b_o, L0_ffn_scores, L0_ffn_expert_weights, L0_ffn_expert_indices, L0_ffn_w1, L0_ffn_w2, L0_ffn_bias, L1_xattn_Wq, L1_xattn_Wk, L1_xattn_Wv, L1_xattn_Wo, L1_ffn_prototypes, L1_ffn_B, L1_ffn_A, L1_ffn_bias, L1_ffn_temp):
    import jax
    import jax.numpy as jnp

    def _L0_xattn_ref(q, k, v, w_q, b_q, w_k, b_k, w_v, b_v, w_o, b_o):
        import jax, jax.numpy as jnp
        import numpy as np
        D_MODEL = 256
        N_HEAD = 16

        def _split_heads(x):
            B, S, D = x.shape
            return x.reshape(B, S, N_HEAD, D // N_HEAD).transpose(0, 2, 1, 3)
        qh = _split_heads(q @ w_q.T + b_q)
        kh = _split_heads(k @ w_k.T + b_k)
        vh = _split_heads(v @ w_v.T + b_v)
        d_k = qh.shape[-1]
        scores = jnp.einsum('bhqd,bhkd->bhqk', qh, kh) / jnp.sqrt(jnp.float32(d_k))
        attn = jax.nn.softmax(scores, axis=-1)
        out = jnp.einsum('bhqk,bhkd->bhqd', attn, vh)
        B, H, S, d = out.shape
        out = out.transpose(0, 2, 1, 3).reshape(B, S, H * d)
        return out @ w_o.T + b_o

    def _L0_ffn_ref(x, scores, expert_weights, expert_indices, w1, w2, bias):
        import jax, jax.numpy as jnp
        import numpy as np
        SL, BS, HS, FF, E, TOPK = (512, 2, 256, 1024, 8, 2)
        sl, bs, hs = x.shape
        n_exp = w1.shape[0]
        top_k = expert_indices.shape[-1]
        xf = x.reshape(-1, hs)
        flat_idx = expert_indices.reshape(-1)
        flat_w = expert_weights.reshape(-1)
        order = jnp.argsort(flat_idx)
        tok = order // top_k
        tokens_per_expert = jnp.bincount(flat_idx, length=n_exp).astype(jnp.int32)
        xs = xf[tok]
        h = jax.nn.gelu(jax.lax.ragged_dot(xs, w1, tokens_per_expert), approximate=False)
        ys = jax.lax.ragged_dot(h, w2, tokens_per_expert)
        ys = ys * flat_w[order][:, None]
        out = jnp.zeros_like(xf).at[tok].add(ys)
        return out.reshape(sl, bs, hs) + bias

    def _L1_xattn_ref(query_input, key_input, value_input, Wq, Wk, Wv, Wo):
        import jax, jax.numpy as jnp
        import numpy as np
        q = jnp.einsum('bsd,dhk->bshk', query_input, Wq)
        k = jnp.einsum('bsd,dhk->bshk', key_input, Wk)
        v = jnp.einsum('bsd,dhk->bshk', value_input, Wv)
        depth = Wq.shape[-1]
        q = q * depth ** (-0.5)
        logits = jnp.einsum('bthk,bfhk->bhft', k, q)
        weights = jax.nn.softmax(logits, axis=-1)
        ctx = jnp.einsum('bhft,bthk->bfhk', weights, v)
        return jnp.einsum('bfhk,hkd->bfd', ctx, Wo)

    def _L1_ffn_ref(x, prototypes, B, A, bias, temp):
        import jax, jax.numpy as jnp
        import numpy as np
        IN_DIM, OUT_DIM, N_PROTO, RANK = (256, 256, 32, 16)
        lead = x.shape[:-1]
        xf = x.reshape(-1, IN_DIM)
        x2 = jnp.sum(xf * xf, axis=1, keepdims=True)
        p2 = jnp.sum(prototypes * prototypes, axis=1)
        d2 = x2 + p2[None, :] - 2.0 * (xf @ prototypes.T)
        dists = jnp.sqrt(jnp.maximum(d2, 0.0))
        t = jnp.maximum(jnp.abs(temp), 0.1)
        w = jax.nn.softmax(-dists / t, axis=1)
        topw, topi = jax.lax.top_k(w, 2)
        topw = topw / jnp.sum(topw, axis=1, keepdims=True)
        out = jnp.zeros((xf.shape[0], OUT_DIM), dtype=xf.dtype)
        for tslot in range(2):
            idx = topi[:, tslot]
            wt = topw[:, tslot:tslot + 1]
            h = jnp.einsum('nri,ni->nr', B[idx], xf)
            y = jnp.einsum('nor,nr->no', A[idx], h) + bias[idx]
            out = out + wt * y
        return out.reshape(*lead, OUT_DIM)
    x = x + jnp.tanh(g_xattn[0]) * _L0_xattn_ref(_layernorm(x, axis=-1), ctx_1024, ctx_1024, L0_xattn_w_q, L0_xattn_b_q, L0_xattn_w_k, L0_xattn_b_k, L0_xattn_w_v, L0_xattn_b_v, L0_xattn_w_o, L0_xattn_b_o)
    x = x + jnp.tanh(g_ffn[0]) * _L0_ffn_ref(_layernorm(x, axis=-1), L0_ffn_scores, L0_ffn_expert_weights, L0_ffn_expert_indices, L0_ffn_w1, L0_ffn_w2, L0_ffn_bias)
    x = x + jnp.tanh(g_xattn[1]) * _L1_xattn_ref(_layernorm(x, axis=-1), ctx_1024, ctx_1024, L1_xattn_Wq, L1_xattn_Wk, L1_xattn_Wv, L1_xattn_Wo)
    x = x + jnp.tanh(g_ffn[1]) * _L1_ffn_ref(_layernorm(x, axis=-1), L1_ffn_prototypes, L1_ffn_B, L1_ffn_A, L1_ffn_bias, L1_ffn_temp)
    return x

_drawn_inputs = setup_inputs


def setup_inputs(seed=0):
    import zlib

    import numpy as np

    out = dict(_drawn_inputs(seed))
    spreads = {'g_ffn': (-1.0, 0.6),
     'L0_xattn_b_q': (0.0, 0.423),
     'L0_xattn_b_k': (0.0, 0.8),
     'L0_xattn_b_v': (0.0, 0.1),
     'L0_xattn_b_o': (0.0, 0.1),
     'L0_ffn_bias': (0.0, 0.1),
     'L1_ffn_bias': (0.0, 0.1)}
    factors = {'L1_xattn_Wq': 2.909, 'L1_xattn_Wk': 2.921, 'L1_ffn_B': 4.282, 'L1_ffn_A': 4.292}
    for name, (base, spread) in spreads.items():
        noise = np.random.default_rng([zlib.crc32(name.encode()), seed]).standard_normal(out[name].shape)
        drawn = base * np.exp(spread * noise) if base else spread * noise
        out[name] = jnp.asarray(drawn.astype(out[name].dtype))
    for name, factor in factors.items():
        out[name] = (out[name] * factor).astype(out[name].dtype)
    return out
```

```python
import concourse.bass as bass
from concourse import mybir
from contextlib import ExitStack

FP32 = mybir.dt.float32
F32R = mybir.dt.float32r
I32 = mybir.dt.int32
U32 = mybir.dt.uint32
ALU = mybir.AluOpType
ACT = mybir.ActivationFunctionType
AX = mybir.AxisListType

P = 128
NB, SEQ, D = 64, 256, 256
DC = D // P
TPB = SEQ // P
NT = NB * TPB
KEYS = 77
KPAD = KEYS + KEYS % 2
H = 16
SC = H * KEYS
BANK = 512
WORK = 3
EPS = 1e-5
TINY = 1e-30
NPROTO, RANK = 32, 16
LOW = NPROTO * RANK
LC = LOW // P
E, TOPK, FF, MOE_T = 8, 2, 1024, 1024
FC = FF // P
MOE_TILES = MOE_T // P
LN_EXP_TABLES = 6


def need(eng, sem, value):
    if not isinstance(value, int) or value > 0:
        eng.wait_ge(sem, value)


def live(t, n):
    return not isinstance(t, int) or 0 <= t < n


class Steps:

    def __init__(self, eng, sem, turn, per):
        self.eng, self.sem, self.base, self.per, self.k = eng, sem, turn * per, per, 0

    def __call__(self, ins):
        self.k += 1
        assert self.k <= self.per
        ins.then_inc(self.sem, 1)
        self.eng.wait_ge(self.sem, self.base + self.k)


class Ring:

    def __init__(self, uses, banks, first, last, steady):
        self.banks, self.steady = banks, steady
        self.flat, self.at_use = [], {}
        for i in range(first, last):
            for name in uses(i):
                self.at_use[i, name] = len(self.flat)
                self.flat.append((i, name))
        self.per = len(uses(steady))
        assert self.per % banks == 0
        before = [self.flat[self.at_use[i, uses(i)[0]] - banks:self.at_use[i, uses(i)[0]]] for i in (steady - 1, steady)]
        assert [n for _, n in before[0]] == [n for _, n in before[1]]

    def fill(self, i, name):
        n = self.at_use[i if isinstance(i, int) else self.steady, name]
        k = n // self.banks + 1
        return n % self.banks, k if isinstance(i, int) else (i - self.steady) * (self.per // self.banks) + k

    def before(self, i, name):
        n = self.at_use[i if isinstance(i, int) else self.steady, name] - self.banks
        if n < 0:
            return None
        at, what = self.flat[n]
        return (at if isinstance(i, int) else i + (at - self.steady)), what


def load_ln_exp_tables(nc):
    nc.scalar.add_instruction(mybir.InstLoadActFuncSet(
        act_func_set_id=LN_EXP_TABLES, name=nc.get_next_instruction_name(),
        engine=mybir.EngineType.Activation, ins=[], outs=[]))


def matmul3(nc, out, lhs, rhs, start, stop):
    nc.tensor.matmul(out, lhs[0], rhs[0], start=start, stop=False)
    nc.tensor.matmul(out, lhs[0], rhs[1], start=False, stop=False)
    return nc.tensor.matmul(out, lhs[1], rhs[0], start=False, stop=stop)


def row(ap, parts, n):
    return ap.rearrange("(a n) -> a n", a=1).broadcast_to([parts, n])


def plain(ap):
    return ap.bitcast(FP32)


def attention_phase(nc, ctx, psum, const, name, src, dst, context, head, weights, q_scale, q_bias, k_bias,
                    v_bias, residual_row, norm_residual, ffn):
    wq, wk, wv, wo = weights
    ident, eps = const["ident"], const["eps"]
    HB = P // head
    BLK = H // HB
    QU = max(2, BLK // 2)
    QB = BLK // QU
    KU = max(1, BLK // 4)
    KB = BLK // KU
    VU = max(1, H * head // BANK)
    VC = H * head // VU
    OU = max(1, BLK // 4)
    OB = BLK // OU
    SLOTS = 2 * TPB
    LAG = 3 if ffn else 1
    END = NB + (LAG + TPB - 1) // TPB
    LN_STEPS, LN2_STEPS, TOP_STEPS = 5, 7, 12

    sb = lambda n, s, d=FP32: ctx.enter_context(nc.sbuf_tensor(f"{name}_{n}", s, d))
    sem = lambda n: ctx.enter_context(nc.semaphore(f"{name}_{n}"))
    pair = lambda n, s: (sb(n + "_hi", s, F32R), sb(n + "_lo", s, F32R))

    x_sb = [sb(f"x{p}", [P, TPB, D]) for p in range(2)]
    res = [sb(f"res{p}", [P, TPB, D]) for p in range(2)]
    ctx_sb = [sb(f"ctx{p}", [KEYS, D]) for p in range(2)]
    ctxT = pair("ctxT", [P, DC, KPAD])
    xn = sb("xn", [P, TPB, D])
    xnT = pair("xnT", [P, DC, SEQ])
    qT = sb("qT", [P, BLK, SEQ])
    kT = sb("kT", [P, BLK, KEYS])
    kbd = [sb(f"kbd{p}", [P, BLK, HB, KEYS]) for p in range(2)]
    v_sb = [sb(f"v{p}", [KEYS, H * head]) for p in range(2)]
    prob = [sb(f"prob{p}", [P, SC]) for p in range(2)]
    probT = sb("probT", [KEYS, H, P])
    smax, ssum, rsum = sb("smax", [P, H]), sb("ssum", [P, H]), sb("rsum", [P, H])
    att = sb("att", [P, H * head])
    attT = pair("attT", [P, BLK, P])
    y_sb = [sb(f"y{s}", [P, D]) for s in range(SLOTS)]
    stats, mv = sb("stats", [P, TPB, 6]), sb("mv", [P, TPB, 2])
    lnv, rstd, nwt = sb("lnv", [P, TPB]), sb("rstd", [P, TPB]), sb("nwt", [P, TPB])
    idle = sb("idle", [P, 1])
    mask = sb("mask", [P, HB])
    if ffn:
        stats2, mv2 = sb("stats2", [P, 6]), sb("mv2", [P, 2])
        lnv2, rstd2, nwt2 = sb("lnv2", [P, 1]), sb("rstd2", [P, 1]), sb("nwt2", [P, 1])
        yn = sb("yn", [P, D])
        ynT = pair("ynT", [P, DC, P])
        ysq = sb("ysq", [P, 1])
        dots, near = sb("dots", [P, NPROTO]), sb("near", [P, NPROTO])
        top, topi, topf = sb("top", [P, 8]), sb("topi", [P, 8], U32), sb("topf", [P, 2])
        lnd, rdist, dist = sb("lnd", [P, 2]), sb("rdist", [P, 2]), sb("dist", [P, 2])
        dsum, dgap, late, wtop = sb("dsum", [P, 1]), sb("dgap", [P, 1]), sb("late", [P, 1]), sb("wtop", [P, 2])
        pick = sb("pick", [P, 2, NPROTO])
        wsel = sb("wsel", [P, P])
        wselT = sb("wselT", [P, P])
        hw = sb("hw", [P, LOW])
        hwT = pair("hwT", [P, LC, P])

    ps_scores = psum[:, 0:3 * BANK]
    ps_att = psum[:, 3 * BANK:3 * BANK + H * head]
    work = [psum[:, (5 + s) * BANK:(6 + s) * BANK] for s in range(WORK)]

    x_in = [sem(f"x_in{p}") for p in range(2)]
    ctx_in = [sem(f"ctx_in{p}") for p in range(2)]
    out_done = [sem(f"out_done{s}") for s in range(SLOTS)]
    work_full = [sem(f"work_full{s}") for s in range(WORK)]
    mask_step, setup_done, res_ready = sem("mask_step"), sem("setup_done"), sem("res_ready")
    ln_step, ln_stats, ln_log, ln_rough, xn_ready = (
        sem("ln_step"), sem("ln_stats"), sem("ln_log"), sem("ln_rough"), sem("xn_ready"))
    ctx_hi, ctx_ready, xnT_hi, xnT_ready = sem("ctx_hi"), sem("ctx_ready"), sem("xnT_hi"), sem("xnT_ready")
    kT_ready, kbd_ready, v_ready, q_ready = sem("kT_ready"), sem("kbd_ready"), sem("v_ready"), sem("q_ready")
    scores_full, max_done, scores_read, exp_done = (
        sem("scores_full"), sem("max_done"), sem("scores_read"), sem("exp_done"))
    sum_done, recip_done = sem("sum_done"), sem("recip_done")
    probT_ready, att_full, att_ready = sem("probT_ready"), sem("att_full"), sem("att_ready")
    attT_hi, attT_ready, y_ready = sem("attT_hi"), sem("attT_ready"), sem("y_ready")
    if ffn:
        ln2_step, ln2_stats, ln2_log, ln2_rough, yn_ready = (
            sem("ln2_step"), sem("ln2_stats"), sem("ln2_log"), sem("ln2_rough"), sem("yn_ready"))
        ynT_hi, ynT_ready, dots_read = sem("ynT_hi"), sem("ynT_ready"), sem("dots_read")
        top_step, top_found, top_log, top_rough, gap_ready, late_ready, wsel_ready = (
            sem("top_step"), sem("top_found"), sem("top_log"), sem("top_rough"), sem("gap_ready"),
            sem("late_ready"), sem("wsel_ready"))
        hw_ready, hwT_hi, hwT_ready, wselT_ready, out_ready = (
            sem("hw_ready"), sem("hwT_hi"), sem("hwT_ready"), sem("wselT_ready"), sem("out_ready"))
    last_ready = out_ready if ffn else y_ready

    def prep_uses(h, part):
        if h == 0:
            return [["ctxT"], [("k", n) for n in range(KU)], [("v", n) for n in range(VU)]][part]
        return [["xnT"], [("q", n) for n in range(QU // 2)], [("q", n) for n in range(QU // 2, QU)]][part]

    def uses(i):
        if i < 0:
            return [u for h in range(2) for part in range(3) for u in prep_uses(h, part)]
        names = []
        for h in range(TPB):
            t = TPB * i + h
            prep = lambda part: prep_uses(h, part) if i + 1 < NB else []
            of = lambda lag, what: what if live(t - lag, NT) and lag <= LAG else []
            names += of(1, [("probT", h, g) for g in range(4)])
            names += prep(0) if h == 0 else []
            names += of(3, [("low", h)])
            names += of(2, [("ynT", h)])
            names += prep(1) if h == 0 else prep(0)
            names += of(3, [("hwT", h), ("wselT", h)])
            names += of(1, [("attT", h, n) for n in range(OU)])
            names += prep(1) if h == 1 else []
            names += of(2, [("dots", h)])
            names += prep(2)
            names += of(1, [("out", h)])
            names += of(3, [("ffn", h)])
        return names

    ring = Ring(uses, WORK, -1, END, 3)

    def freed(i, use):
        what, h, n = (use + (0, 0))[:3] if isinstance(use, tuple) else (use, 0, 0)
        t = i * TPB + h
        if what == "probT":
            return probT_ready, (t - 1) * 4 + n + 1
        if what == "attT":
            return attT_ready, (t - 1) * OU + n + 1
        if what in ("k", "v", "q"):
            each = {"k": KU, "v": VU, "q": QU}[what]
            return {"k": kT_ready, "v": v_ready, "q": q_ready}[what], (i + 1) * each + h + 1
        if what in ("ctxT", "xnT"):
            return {"ctxT": ctx_ready, "xnT": xnT_ready}[what], i + 2
        if what == "out":
            return y_ready, t
        if what in ("ynT", "dots"):
            return {"ynT": ynT_ready, "dots": dots_read}[what], t - 1
        return {"low": hw_ready, "hwT": hwT_ready, "wselT": wselT_ready, "ffn": out_ready}[what], t - 2

    def bodies(eng, body):
        for i in (0, 1):
            body(i, i % 2, i // 2)
        with eng.Fori(1, NB // 2 - 1) as j:
            body(j * 2, 0, j)
            body(j * 2 + 1, 1, j)
        for i in range(NB - 2, END):
            body(i, i % 2, i // 2)

    block = ctx.enter_context(nc.Block())

    @block.sync
    def _(sp):
        def load(i, p):
            need(sp, xn_ready, i - 1)
            need(sp, res_ready, i - 1)
            sp.dma_start(x_sb[p][:, :, :], src[i]).then_inc(x_in[p], 16)
            need(sp, ctx_ready, i - 1)
            sp.dma_start(ctx_sb[p][:, :], context[i]).then_inc(ctx_in[p], 16)

        def body(i, u, j):
            if live(i + 2, NB):
                load(i + 2, u)
            for h in range(TPB):
                t = i * TPB + h - LAG
                if live(t, NT):
                    slot = (TPB * u + h - LAG) % SLOTS
                    need(sp, last_ready, t + 1)
                    sp.dma_start(dst[t], y_sb[slot][:, :]).then_inc(out_done[slot], 16)

        load(0, 0)
        load(1, 1)
        bodies(sp, body)
        for s in range(SLOTS):
            sp.wait_ge(out_done[s], 16 * (NT // SLOTS))

    @block.gpsimd
    def _(pool):
        pool.memset(mask[:, :], 1.0).then_inc(mask_step, 1)
        pool.wait_ge(mask_step, 1)
        pool.affine_select(out=mask[:, :], in_=mask[:, :], compare_op=ALU.is_ge, fill=0.0, base=0,
                           pattern=[[-head, HB]], channel_multiplier=1).then_inc(mask_step, 1)
        pool.wait_ge(mask_step, 2)
        pool.affine_select(out=mask[:, :], in_=mask[:, :], compare_op=ALU.is_ge, fill=0.0, base=head - 1,
                           pattern=[[head, HB]], channel_multiplier=-1).then_inc(mask_step, 1)
        pool.wait_ge(mask_step, 3)
        for part in ctxT:
            pool.memset(plain(part[:, :, KEYS:KPAD]), 0.0).then_inc(setup_done, 1)
        if ffn:
            pool.memset(wsel[:, :], 0.0).then_inc(setup_done, 1)

        def keys(i, p):
            need(pool, kT_ready, (i + 1) * KU)
            for b in range(BLK):
                last = pool.tensor_tensor(kbd[p][:, b, :, :], kT[:, b, :].unsqueeze(1).broadcast_to([P, HB, KEYS]),
                                          mask[:, :].unsqueeze(2).broadcast_to([P, HB, KEYS]), ALU.mult)
            last.then_inc(kbd_ready, 1)

        def residual(i, p, j):
            need(pool, x_in[p], (j + 1) * 16)
            need(pool, y_ready, (i - 1) * TPB)
            pool.tensor_tensor(res[p][:, :, :], x_sb[p][:, :, :],
                               residual_row[:, :].unsqueeze(1).broadcast_to([P, TPB, D]), ALU.add)\
                .then_inc(res_ready, 1)

        def body(i, u, j):
            if live(i + 1, NB):
                keys(i + 1, 1 - u)
                residual(i + 1, 1 - u, j + u)

        residual(0, 0, 0)
        keys(0, 0)
        bodies(pool, body)

    @block.scalar
    def _(act):
        load_ln_exp_tables(nc)

        def full(i, use):
            s, k = ring.fill(i, use)
            need(act, work_full[s], k)
            return work[s]

        def inverse_deviation(var, log, out, stats_done, log_done, rough_done, turn):
            need(act, stats_done, turn + 1)
            act.activation(log, var, ACT.Ln, bias=eps[:, 0:1]).then_inc(log_done, 1)
            need(act, log_done, turn + 1)
            act.activation(out, log, ACT.Exp, scale=-0.5).then_inc(rough_done, 1)

        def split_hi(i, use, out, cols, done):
            bank = full(i, use)
            act.activation(out, bank[:, 0:cols].rearrange("p (c s) -> p c s", c=out.shape[1]), ACT.Copy)\
                .then_inc(done, 1)

        def prepare(i, p, h, part):
            if h == 0 and part == 0:
                split_hi(i, "ctxT", ctxT[0][:, :, 0:KEYS], DC * KEYS, ctx_hi)
            if h == 0 and part == 1:
                need(act, kbd_ready, i + 1)
                for n in range(KU):
                    bank = full(i, ("k", n))[:, 0:KB * KPAD].rearrange("p (b k) -> p b k", b=KB)[:, :, 0:KEYS]
                    if k_bias is None:
                        last = act.activation(kT[:, n * KB:(n + 1) * KB, :], bank, ACT.Copy)
                    else:
                        for b in range(KB):
                            last = act.activation(kT[:, n * KB + b, :], bank[:, b, :], ACT.Identity,
                                                  bias=k_bias[:, n * KB + b:n * KB + b + 1])
                    last.then_inc(kT_ready, 1)
            if h == 0 and part == 2 and v_bias is None:
                for n in range(VU):
                    bank = full(i, ("v", n))
                    act.activation(v_sb[p][:, n * VC:(n + 1) * VC], bank[0:KEYS, 0:VC], ACT.Copy)\
                        .then_inc(v_ready, 1)
            if h == 1 and part == 0:
                split_hi(i, "xnT", xnT[0][:, :, :], DC * SEQ, xnT_hi)
            if h == 1 and part > 0:
                for n in range(QU // 2 * (part - 1), QU // 2 * part):
                    bank = full(i, ("q", n))[:, 0:QB * SEQ].rearrange("p (b s) -> p b s", b=QB)
                    out = qT[:, n * QB:(n + 1) * QB, :]
                    if q_bias is None:
                        last = act.activation(out, bank, ACT.Copy, scale=q_scale)
                    else:
                        last = act.activation(out, bank, ACT.Identity, scale=q_scale, bias=q_bias[:, n:n + 1])
                    last.then_inc(q_ready, 1)

        def body(i, u, j):
            prep = live(i + 1, NB)
            for h in range(TPB):
                t = i * TPB + h
                if live(t - 1, NT):
                    for g in range(4):
                        bank = full(i, ("probT", h, g))
                        act.activation(probT[:, 4 * g:4 * g + 4, :],
                                       bank[0:KEYS, :].rearrange("p (h s) -> p h s", h=4), ACT.Copy)\
                            .then_inc(probT_ready, 1)
                if live(t, NT):
                    need(act, scores_read, t + 1)
                    act.activation(prob[h][:, :], prob[h][:, :], ACT.Exp).then_inc(exp_done, 1)
                if prep and h == 0:
                    prepare(i, 1 - u, 0, 0)
                if prep and h == 1:
                    inverse_deviation(mv[:, :, 1], lnv[:, :], rstd[:, :], ln_stats, ln_log, ln_rough, i + 1)
                if ffn and live(t - 2, NT):
                    split_hi(i, ("ynT", h), ynT[0][:, :, :], DC * P, ynT_hi)
                if prep:
                    prepare(i, 1 - u, h, 1 - h)
                if ffn and live(t - 3, NT):
                    split_hi(i, ("hwT", h), hwT[0][:, :, :], LC * P, hwT_hi)
                    bank = full(i, ("wselT", h))
                    act.activation(wselT[:, :], bank[:, 0:P], ACT.Copy).then_inc(wselT_ready, 1)
                if live(t - 1, NT):
                    for n in range(OU):
                        split_hi(i, ("attT", h, n), attT[0][:, n * OB:(n + 1) * OB, :], OB * P, attT_hi)
                if prep and h == 1:
                    prepare(i, 1 - u, 1, 1)
                if ffn and live(t - 2, NT):
                    need(act, top_found, t - 1)
                    act.activation(lnd[:, :], top[:, 0:2], ACT.Ln, scale=-1.0).then_inc(top_log, 1)
                    need(act, top_log, t - 1)
                    act.activation(rdist[:, :], lnd[:, :], ACT.Exp, scale=-0.5).then_inc(top_rough, 1)
                if prep:
                    prepare(i, 1 - u, h, 2)
                if ffn and live(t - 1, NT):
                    inverse_deviation(mv2[:, 1:2], lnv2[:, :], rstd2[:, :], ln2_stats, ln2_log, ln2_rough, t - 1)
                if ffn and live(t - 2, NT):
                    need(act, gap_ready, t - 1)
                    act.activation(late[:, :], dgap[:, :], ACT.Exp, scale=ffn["minus_inv_temp"][:, 0:1])\
                        .then_inc(late_ready, 1)

        prepare(-1, 0, 0, 0)
        prepare(-1, 0, 0, 1)
        prepare(-1, 0, 0, 2)
        inverse_deviation(mv[:, :, 1], lnv[:, :], rstd[:, :], ln_stats, ln_log, ln_rough, 0)
        prepare(-1, 0, 1, 0)
        prepare(-1, 0, 1, 1)
        prepare(-1, 0, 1, 2)
        bodies(act, body)

    @block.tensor
    def _(pe):
        def bank_for(i, use):
            before = ring.before(i, use)
            if before is not None:
                need(pe, *freed(*before))
            return work[ring.fill(i, use)[0]]

        def filled(ins, i, use):
            ins.then_inc(work_full[ring.fill(i, use)[0]], 1)

        def prepare(i, p, j, h, part):
            if h == 0 and part == 0:
                need(pe, ctx_in[p], (j + 1) * 16)
                bank = bank_for(i, "ctxT")
                for c in range(DC):
                    last = nc.tensor.transpose(bank[:, c * KEYS:(c + 1) * KEYS], ctx_sb[p][:, c * P:(c + 1) * P],
                                               ident[0:KEYS, 0:KEYS])
                filled(last, i, "ctxT")
            if h == 0 and part == 1:
                need(pe, ctx_ready, i + 2)
                for n in range(KU):
                    bank = bank_for(i, ("k", n))
                    for b in range(KB):
                        at = (n * KB + b) * P
                        for c in range(DC):
                            last = matmul3(nc, bank[:, b * KPAD:(b + 1) * KPAD], [w[:, c, at:at + P] for w in wk],
                                           [a[:, c, :] for a in ctxT], c == 0, c == DC - 1)
                    filled(last, i, ("k", n))
            if h == 0 and part == 2:
                for n in range(VU):
                    bank = bank_for(i, ("v", n))
                    for c in range(DC):
                        last = matmul3(nc, bank[0:KEYS, 0:VC], [a[:, c, 0:KEYS] for a in ctxT],
                                       [w[:, c, n * VC:(n + 1) * VC] for w in wv], c == 0, c == DC - 1)
                    filled(last, i, ("v", n))
            if h == 1 and part == 0:
                need(pe, xn_ready, i + 2)
                bank = bank_for(i, "xnT")
                for c in range(DC):
                    for a in range(TPB):
                        last = nc.tensor.transpose(bank[:, c * SEQ + a * P:c * SEQ + (a + 1) * P],
                                                   xn[:, a, c * P:(c + 1) * P], ident[:, :])
                filled(last, i, "xnT")
            if h == 1 and part > 0:
                need(pe, xnT_ready, i + 2)
                for n in range(QU // 2 * (part - 1), QU // 2 * part):
                    bank = bank_for(i, ("q", n))
                    for b in range(QB):
                        at = (n * QB + b) * P
                        for c in range(DC):
                            last = matmul3(nc, bank[:, b * SEQ:(b + 1) * SEQ], [w[:, c, at:at + P] for w in wq],
                                           [a[:, c, :] for a in xnT], c == 0, c == DC - 1)
                    filled(last, i, ("q", n))

        def scores(i, t, h, u):
            need(pe, kbd_ready, i + 1)
            need(pe, q_ready, (i + 1) * QU)
            need(pe, scores_read, t)
            for b in range(BLK):
                at, end = b * HB * KEYS, (b + 1) * HB * KEYS
                while at < end:
                    to = min(end, (at // BANK + 1) * BANK)
                    last = nc.tensor.matmul(ps_scores[:, at:to], qT[:, b, h * P:(h + 1) * P],
                                            kbd[u][:, b, :, :].rearrange("p a k -> p (a k)")
                                            [:, at - b * HB * KEYS:to - b * HB * KEYS], start=True, stop=True)
                    at = to
            last.then_inc(scores_full, 1)

        def values(i, t, h, v):
            need(pe, probT_ready, (t + 1) * 4)
            need(pe, v_ready, (i + 1) * VU)
            need(pe, att_ready, t)
            for a in range(H):
                last = nc.tensor.matmul(ps_att[:, a * head:(a + 1) * head], probT[:, a, :],
                                        v[:, a * head:(a + 1) * head], start=True, stop=True)
            last.then_inc(att_full, 1)

        def body(i, u, j):
            prep = lambda h, part: prepare(i, 1 - u, j + u, h, part) if live(i + 1, NB) else None
            for h in range(TPB):
                t = i * TPB + h
                past = u if h else 1 - u
                if live(t, NT):
                    scores(i, t, h, u)
                if live(t - 1, NT):
                    need(pe, exp_done, t)
                    for g in range(4):
                        bank = bank_for(i, ("probT", h, g))
                        for a in range(4):
                            at = (4 * g + a) * KEYS
                            last = nc.tensor.transpose(bank[0:KEYS, a * P:(a + 1) * P],
                                                       prob[1 - h][:, at:at + KEYS], ident[:, :])
                        filled(last, i, ("probT", h, g))
                if h == 0:
                    prep(0, 0)
                if ffn and live(t - 3, NT):
                    bank = bank_for(i, ("low", h))
                    for c in range(DC):
                        last = matmul3(nc, bank[:, 0:LOW], [a[:, c, :] for a in ynT],
                                       [w[:, c, :] for w in ffn["down"]], c == 0, c == DC - 1)
                    filled(last, i, ("low", h))
                if live(t - 1, NT):
                    values(i - 1 + h, t - 1, 1 - h, v_sb[past])
                if ffn and live(t - 2, NT):
                    need(pe, yn_ready, t - 1)
                    bank = bank_for(i, ("ynT", h))
                    for c in range(DC):
                        last = nc.tensor.transpose(bank[:, c * P:(c + 1) * P], yn[:, c * P:(c + 1) * P], ident[:, :])
                    filled(last, i, ("ynT", h))
                prep(h, 1 - h)
                if ffn and live(t - 3, NT):
                    need(pe, hw_ready, t - 2)
                    bank = bank_for(i, ("hwT", h))
                    for c in range(LC):
                        last = nc.tensor.transpose(bank[:, c * P:(c + 1) * P], hw[:, c * P:(c + 1) * P], ident[:, :])
                    filled(last, i, ("hwT", h))
                    bank = bank_for(i, ("wselT", h))
                    filled(nc.tensor.transpose(bank[:, 0:P], wsel[:, :], ident[:, :]), i, ("wselT", h))
                if live(t - 1, NT):
                    need(pe, att_ready, t)
                    for n in range(OU):
                        bank = bank_for(i, ("attT", h, n))
                        for b in range(OB):
                            at = (n * OB + b) * P
                            last = nc.tensor.transpose(bank[:, b * P:(b + 1) * P], att[:, at:at + P], ident[:, :])
                        filled(last, i, ("attT", h, n))
                if h == 1:
                    prep(1, 1)
                if ffn and live(t - 2, NT):
                    need(pe, ynT_ready, t - 1)
                    bank = bank_for(i, ("dots", h))
                    for c in range(DC):
                        last = matmul3(nc, bank[:, 0:NPROTO], [a[:, c, :] for a in ynT],
                                       [w[:, c, :] for w in ffn["protoT"]], c == 0, c == DC - 1)
                    filled(last, i, ("dots", h))
                prep(h, 2)
                if live(t - 1, NT):
                    need(pe, attT_ready, t * OU)
                    bank = bank_for(i, ("out", h))
                    for b in range(BLK):
                        last = matmul3(nc, bank[:, 0:D], [a[:, b, :] for a in attT], [w[:, b, :] for w in wo],
                                       b == 0, b == BLK - 1)
                    filled(last, i, ("out", h))
                if ffn and live(t - 3, NT):
                    need(pe, hwT_ready, t - 2)
                    need(pe, wselT_ready, t - 2)
                    bank = bank_for(i, ("ffn", h))
                    for c in range(LC):
                        matmul3(nc, bank[:, 0:D], [a[:, c, :] for a in hwT], [w[:, c, :] for w in ffn["up"]],
                                c == 0, False)
                    filled(nc.tensor.matmul(bank[:, 0:D], wselT[:, :], ffn["bias"][:, :], start=False, stop=True),
                           i, ("ffn", h))

        need(pe, setup_done, 3 if ffn else 2)
        for h in range(2):
            for part in range(3):
                prepare(-1, 0, 0, h, part)
        bodies(pe, body)

    @block.vector
    def _(dve):
        def full(i, use):
            s, k = ring.fill(i, use)
            need(dve, work_full[s], k)
            return work[s]

        def hold(sem_, value):
            need(dve, sem_, value)
            nc.vector.memset(idle[:, :], 0.0)

        def split_lo(i, use, hi, lo, cols, hi_done, turn, done):
            bank = full(i, use)
            need(dve, hi_done, turn)
            nc.vector.tensor_tensor(lo, bank[:, 0:cols].rearrange("p (c s) -> p c s", c=hi.shape[1]), plain(hi),
                                    ALU.subtract).then_inc(done, 1)

        def refine(step, var, rough, tmp):
            step(nc.vector.tensor_tensor(tmp, rough, rough, ALU.mult))
            step(nc.vector.scalar_tensor_tensor(out=tmp, in0=var, scalar=EPS, in1=tmp, op0=ALU.add, op1=ALU.mult))
            step(nc.vector.tensor_scalar(tmp, tmp, -0.5, 1.5, ALU.mult, ALU.add))
            step(nc.vector.tensor_tensor(rough, rough, tmp, ALU.mult))

        def norm_stats(i, p, j):
            source = res[p] if norm_residual else x_sb[p]
            if norm_residual:
                need(dve, res_ready, i + 1)
            else:
                need(dve, x_in[p], (j + 1) * 16)
            step = Steps(dve, ln_step, i, LN_STEPS)
            for a in range(TPB):
                last = nc.vector.bn_stats(stats[:, a, :], source[:, a, :])
                if a == TPB - 1:
                    step(last)
            nc.vector.memset(idle[:, :], 0.0)
            for a in range(TPB):
                last = nc.vector.bn_aggr(mv[:, a, :], stats[:, a, :])
            last.then_inc(ln_stats, 1)
            return step

        def norm_apply(i, p, step):
            source = res[p] if norm_residual else x_sb[p]
            need(dve, ln_rough, i + 1)
            need(dve, ln_stats, i + 1)
            refine(step, mv[:, :, 1], rstd[:, :], nwt[:, :])
            for a in range(TPB):
                last = nc.vector.tensor_scalar(xn[:, a, :], source[:, a, :], mv[:, a, 0:1], rstd[:, a:a + 1],
                                               ALU.subtract, ALU.mult)
            last.then_inc(xn_ready, 1)

        def softmax_sums(t, h):
            need(dve, exp_done, t + 1)
            nc.vector.reduce_sum(ssum[:, :], prob[h][:, :].rearrange("p (h k) -> p h k", h=H), AX.X)\
                .then_inc(sum_done, 1)
            need(dve, sum_done, t + 1)
            nc.vector.reciprocal(rsum[:, :], ssum[:, :]).then_inc(recip_done, 1)

        def shift_scores(t, h):
            scores = ps_scores[:, 0:SC].rearrange("p (h k) -> p h k", h=H)
            need(dve, scores_full, t + 1)
            nc.vector.reduce_max(smax[:, :], scores, AX.X).then_inc(max_done, 1)
            need(dve, max_done, t + 1)
            nc.vector.tensor_tensor(prob[h][:, :].rearrange("p (h k) -> p h k", h=H), scores,
                                    smax[:, :].unsqueeze(2).broadcast_to([P, H, KEYS]), ALU.subtract)\
                .then_inc(scores_read, 1)

        def biased_values(i, p):
            for n in range(VU):
                bank = full(i, ("v", n))
                nc.vector.tensor_tensor(v_sb[p][:, n * VC:(n + 1) * VC], bank[0:KEYS, 0:VC],
                                        v_bias[:, n * VC:(n + 1) * VC], ALU.add).then_inc(v_ready, 1)

        def nearest(i, t, h):
            bank = full(i, ("dots", h))
            step = Steps(dve, top_step, t, TOP_STEPS)
            nc.vector.scalar_tensor_tensor(out=dots[:, :], in0=bank[:, 0:NPROTO], scalar=2.0,
                                           in1=ffn["proto_sq"][:, :], op0=ALU.mult, op1=ALU.subtract)\
                .then_inc(dots_read, 1)
            need(dve, dots_read, t + 1)
            step(nc.vector.tensor_scalar(near[:, :], dots[:, :], ysq[:, 0:1], -TINY, ALU.subtract, ALU.min))
            nc.vector.memset(idle[:, :], 0.0)
            nc.vector.max(top[:, :], near[:, :]).then_inc(top_found, 1)
            hold(top_found, t + 1)
            nc.vector.max_index(topi[:, :], top[:, :], near[:, :]).then_inc(top_step, 1)
            step.k += 1
            return step

        def distance_gap(t, step):
            dve.wait_ge(top_step, step.base + step.k)
            step(nc.vector.tensor_copy(topf[:, :], topi[:, 0:2]))
            need(dve, top_rough, t + 1)
            step(nc.vector.tensor_tensor(dist[:, :], top[:, 0:2], rdist[:, :], ALU.mult))
            step(nc.vector.tensor_tensor(dsum[:, :], dist[:, 0:1], dist[:, 1:2], ALU.add))
            step(nc.vector.reciprocal(dsum[:, :], dsum[:, :]))
            step(nc.vector.tensor_tensor(dgap[:, :], top[:, 1:2], top[:, 0:1], ALU.subtract))
            nc.vector.tensor_tensor(dgap[:, :], dgap[:, :], dsum[:, :], ALU.mult).then_inc(gap_ready, 1)

        def choose(t, step):
            need(dve, late_ready, t + 1)
            step(nc.vector.tensor_scalar(wtop[:, 0:1], late[:, :], 1.0, None, ALU.add))
            step(nc.vector.reciprocal(wtop[:, 0:1], wtop[:, 0:1]))
            step(nc.vector.tensor_tensor(wtop[:, 1:2], late[:, :], wtop[:, 0:1], ALU.mult))
            for k in range(2):
                step(nc.vector.tensor_scalar(pick[:, k, :], const["iota"][:, :], topf[:, k:k + 1], wtop[:, k:k + 1],
                                             ALU.is_equal, ALU.mult))
            nc.vector.tensor_tensor(wsel[:, 0:NPROTO], pick[:, 0, :], pick[:, 1, :], ALU.add).then_inc(wsel_ready, 1)

        def body(i, u, j):
            prep = live(i + 1, NB)
            for h in range(TPB):
                t = i * TPB + h
                slot = lambda lag: (TPB * u + h - lag) % SLOTS
                if live(t - 1, NT):
                    softmax_sums(t - 1, 1 - h)
                if live(t, NT):
                    shift_scores(t, h)
                if prep and h == 0:
                    split_lo(i, "ctxT", ctxT[0][:, :, 0:KEYS], ctxT[1][:, :, 0:KEYS], DC * KEYS, ctx_hi, i + 2,
                             ctx_ready)
                if prep and h == 1:
                    norm_step = norm_stats(i + 1, 1 - u, j + u)
                if ffn and live(t - 3, NT):
                    bank = full(i, ("low", h))
                    need(dve, wsel_ready, t - 2)
                    nc.vector.tensor_tensor(hw[:, :].rearrange("p (n r) -> p n r", n=NPROTO),
                                            bank[:, 0:LOW].rearrange("p (n r) -> p n r", n=NPROTO),
                                            wsel[:, 0:NPROTO].unsqueeze(2).broadcast_to([P, NPROTO, RANK]),
                                            ALU.mult).then_inc(hw_ready, 1)
                if prep and h == 1:
                    norm_apply(i + 1, 1 - u, norm_step)
                if live(t - 1, NT):
                    need(dve, att_full, t)
                    need(dve, recip_done, t)
                    nc.vector.tensor_tensor(att[:, :].rearrange("p (h k) -> p h k", h=H),
                                            ps_att.rearrange("p (h k) -> p h k", h=H),
                                            rsum[:, :].unsqueeze(2).broadcast_to([P, H, head]), ALU.mult)\
                        .then_inc(att_ready, 1)
                if ffn and live(t - 2, NT):
                    split_lo(i, ("ynT", h), ynT[0][:, :, :], ynT[1][:, :, :], DC * P, ynT_hi, t - 1, ynT_ready)
                if prep and h == 1:
                    split_lo(i, "xnT", xnT[0][:, :, :], xnT[1][:, :, :], DC * SEQ, xnT_hi, i + 2, xnT_ready)
                if ffn and live(t - 3, NT):
                    split_lo(i, ("hwT", h), hwT[0][:, :, :], hwT[1][:, :, :], LC * P, hwT_hi, t - 2, hwT_ready)
                if live(t - 1, NT):
                    for n in range(OU):
                        part = slice(n * OB, (n + 1) * OB)
                        split_lo(i, ("attT", h, n), attT[0][:, part, :], attT[1][:, part, :], OB * P, attT_hi,
                                 (t - 1) * OU + n + 1, attT_ready)
                if ffn and live(t - 2, NT):
                    top_chain = nearest(i, t - 2, h)
                if prep and h == 0 and v_bias is not None:
                    biased_values(i, 1 - u)
                if live(t - 1, NT):
                    bank = full(i, ("out", h))
                    need(dve, res_ready, i + h)
                    need(dve, out_done[slot(1)], tile_turn(u, j, h - 1) * 16)
                    y = y_sb[slot(1)]
                    nc.vector.tensor_tensor(y[:, :], bank[:, 0:D], res[(u if h else 1 - u)][:, 1 - h, :], ALU.add)\
                        .then_inc(y_ready, 1)
                if ffn and live(t - 1, NT):
                    step2 = Steps(dve, ln2_step, t - 1, LN2_STEPS)
                    need(dve, y_ready, t)
                    step2(nc.vector.bn_stats(stats2[:, :], y[:, :]))
                    nc.vector.memset(idle[:, :], 0.0)
                    nc.vector.bn_aggr(mv2[:, :], stats2[:, :]).then_inc(ln2_stats, 1)
                if ffn and live(t - 2, NT):
                    distance_gap(t - 2, top_chain)
                if ffn and live(t - 3, NT):
                    bank = full(i, ("ffn", h))
                    y3 = y_sb[slot(3)]
                    nc.vector.tensor_tensor(y3[:, :], bank[:, 0:D], y3[:, :], ALU.add).then_inc(out_ready, 1)
                if ffn and live(t - 1, NT):
                    need(dve, ln2_rough, t)
                    need(dve, ln2_stats, t)
                    refine(step2, mv2[:, 1:2], rstd2[:, :], nwt2[:, :])
                    step2(nc.vector.scalar_tensor_tensor(out=nwt2[:, :], in0=rstd2[:, :], scalar=float(D),
                                                         in1=rstd2[:, :], op0=ALU.mult, op1=ALU.mult))
                    step2(nc.vector.tensor_tensor(ysq[:, :], nwt2[:, :], mv2[:, 1:2], ALU.mult))
                    nc.vector.tensor_scalar(yn[:, :], y[:, :], mv2[:, 0:1], rstd2[:, 0:1],
                                            ALU.subtract, ALU.mult).then_inc(yn_ready, 1)
                if ffn and live(t - 2, NT):
                    choose(t - 2, top_chain)

        def tile_turn(u, j, back):
            return j if TPB * u + back >= 0 else j - 1

        if ffn:
            dve.wait_ge(setup_done, 3)
        split_lo(-1, "ctxT", ctxT[0][:, :, 0:KEYS], ctxT[1][:, :, 0:KEYS], DC * KEYS, ctx_hi, 1, ctx_ready)
        if v_bias is not None:
            biased_values(-1, 0)
        first = norm_stats(0, 0, 0)
        norm_apply(0, 0, first)
        split_lo(-1, "xnT", xnT[0][:, :, :], xnT[1][:, :, :], DC * SEQ, xnT_hi, 1, xnT_ready)
        bodies(dve, body)


def split(nc, act, hi, lo, src, scale, hi_done, turn, lo_done):
    if act:
        func = ACT.Copy if isinstance(scale, float) else ACT.Identity
        nc.scalar.activation(hi, src, func, scale=scale).then_inc(hi_done, 1)
    else:
        nc.vector.wait_ge(hi_done, turn)
        nc.vector.scalar_tensor_tensor(out=lo, in0=src, scalar=scale, in1=plain(hi), op0=ALU.mult,
                                       op1=ALU.subtract).then_inc(lo_done, 1)


def constants(nc, ctx, g_xattn, g_ffn):
    sb = lambda n, s, d=FP32: ctx.enter_context(nc.sbuf_tensor(n, s, d))
    sem = lambda n: ctx.enter_context(nc.semaphore(n))
    ident, iota, eps, gates = sb("ident", [P, P]), sb("iota", [P, NPROTO]), sb("eps", [P, 1]), sb("gates", [P, 4])
    ident_zero, gates_in = sem("ident_zero"), sem("gates_in")
    with nc.Block() as block:
        @block.sync
        def _(sp):
            sp.dma_start(gates[:, 0:2], row(g_xattn, P, 2)).then_inc(gates_in, 16)
            sp.dma_start(gates[:, 2:4], row(g_ffn, P, 2)).then_inc(gates_in, 16)

        @block.gpsimd
        def _(pool):
            pool.memset(ident[:, :], 0.0).then_inc(ident_zero, 1)
            pool.memset(eps[:, :], EPS)
            pool.wait_ge(ident_zero, 1)
            pool.affine_select(out=ident[:, :], in_=ident[:, :], compare_op=ALU.not_equal, fill=1.0, base=0,
                               pattern=[[-1, P]], channel_multiplier=1)
            pool.iota(iota[:, :], [[1, NPROTO]], base=0, channel_multiplier=0, allow_small_or_imprecise_dtypes=True)

        @block.scalar
        def _(act):
            act.wait_ge(gates_in, 32)
            act.activation(gates[:, :], gates[:, :], ACT.Tanh)
    return {"ident": ident, "iota": iota, "eps": eps, "gates": gates}


def layer0_weights(nc, ctx, psum, const, w_q, b_q, w_k, b_k, w_v, b_v, w_o, b_o):
    sb = lambda n, s, d=FP32: ctx.enter_context(nc.sbuf_tensor(f"w0_{n}", s, d))
    sem = lambda n: ctx.enter_context(nc.semaphore(f"w0_{n}"))
    wT = [(sb(f"{n}T_hi", [P, DC, D], F32R), sb(f"{n}T_lo", [P, DC, D], F32R)) for n in "qkvo"]
    bq, bk = sb("bq", [P, DC]), sb("bk", [P, DC])
    bv, bo = sb("bv", [KEYS, D]), sb("bo", [P, D])
    raw_in = [sem(f"raw_in{n}") for n in range(4)]
    bias_in, turned, hi_done, lo_done = sem("bias_in"), sem("turned"), sem("hi_done"), sem("lo_done")
    gate = const["gates"][:, 0:1]
    q_scale = float(D // H) ** -0.5
    scales = [1.0, 1.0, 1.0, gate]
    with ExitStack() as inner:
        raw = [inner.enter_context(nc.sbuf_tensor(f"w0_raw{n}", [P, DC, D], FP32)) for n in range(4)]
        block = inner.enter_context(nc.Block())
        bank = lambda n: psum[:, n * BANK:(n + 1) * BANK].rearrange("p (c o) -> p c o", c=DC)

        @block.sync
        def _(sp):
            for n, w in enumerate((w_q, w_k, w_v, w_o)):
                sp.dma_start(raw[n][:, :, :], w.rearrange("(a p) d -> p a d", p=P)).then_inc(raw_in[n], 16)
            with nc.allow_non_contiguous_dma("biases, one value per partition"):
                sp.dma_start(bq[:, :], b_q.rearrange("(c p) -> p c", p=P)).then_inc(bias_in, 16)
                sp.dma_start(bk[:, :], b_k.rearrange("(c p) -> p c", p=P)).then_inc(bias_in, 16)
            sp.dma_start(bv[:, :], row(b_v, KEYS, D)).then_inc(bias_in, 16)
            sp.dma_start(bo[:, :], row(b_o, P, D)).then_inc(bias_in, 16)

        @block.tensor
        def _(pe):
            for n in range(4):
                pe.wait_ge(raw_in[n], 16)
                for c in range(DC):
                    for a in range(DC):
                        last = nc.tensor.transpose(bank(n)[:, c, a * P:(a + 1) * P], raw[n][:, a, c * P:(c + 1) * P],
                                                   const["ident"][:, :])
                last.then_inc(turned, 1)

        @block.scalar
        def _(act):
            for n in range(4):
                act.wait_ge(turned, n + 1)
                split(nc, True, wT[n][0][:, :, :], wT[n][1][:, :, :], bank(n), scales[n], hi_done, n + 1, lo_done)
            act.wait_ge(bias_in, 64)
            act.activation(bq[:, :], bq[:, :], ACT.Copy, scale=q_scale)

        @block.vector
        def _(dve):
            for n in range(4):
                split(nc, False, wT[n][0][:, :, :], wT[n][1][:, :, :], bank(n), scales[n], hi_done, n + 1, lo_done)
            dve.wait_ge(bias_in, 64)
            nc.vector.tensor_scalar(bo[:, :], bo[:, :], gate, None, ALU.mult)
    return wT, q_scale, bq, bk, bv, bo


def layer1_weights(nc, ctx, psum, const, w_q, w_k, w_v, w_o, protos, low_b, low_a, low_bias, temp, bias0):
    sb = lambda n, s, d=FP32: ctx.enter_context(nc.sbuf_tensor(f"w1_{n}", s, d))
    sem = lambda n: ctx.enter_context(nc.semaphore(f"w1_{n}"))
    pair = lambda n, s: (sb(n + "_hi", s, F32R), sb(n + "_lo", s, F32R))
    W = H * 64
    wq, wk, wv = pair("q", [P, DC, W]), pair("k", [P, DC, W]), pair("v", [P, DC, W])
    wo = pair("o", [P, W // P, D])
    downT, upT, protoT = pair("downT", [P, DC, LOW]), pair("upT", [P, LC, D]), pair("protoT", [P, DC, NPROTO])
    low_bias_sb, proto_sq = sb("low_bias", [P, D]), sb("proto_sq", [P, NPROTO])
    mit, bias0_row = sb("minus_inv_temp", [P, 1]), sb("bias0", [P, D])
    gates = const["gates"]
    raw_in = [sem(f"raw_in{n}") for n in range(7)]
    small_in, bias_zero, turned, hi_done, lo_done, sq_done, sq_full, step_sem, ones_set = (
        sem("small_in"), sem("bias_zero"), sem("turned"), sem("hi_done"), sem("lo_done"), sem("sq_done"),
        sem("sq_full"), sem("step"), sem("ones_set"))
    with ExitStack() as inner:
        tmp = lambda n, s: inner.enter_context(nc.sbuf_tensor(f"w1_{n}", s, FP32))
        raw = [tmp(f"raw{n}", [P, DC, W]) for n in range(3)] + [tmp("raw3", [P, W // P, D])]
        raw_p, raw_b, raw_a = tmp("raw_p", [NPROTO, D]), tmp("raw_b", [P, LC, D]), tmp("raw_a", [P, DC, LOW])
        sq, ones, neg = tmp("sq", [P, DC, NPROTO]), tmp("ones", [P, P]), tmp("neg", [P, 1])
        block = inner.enter_context(nc.Block())
        ident = const["ident"]
        cols = lambda n, c, k=1: psum[:, n * BANK:n * BANK + c * k].rearrange("p (c o) -> p c o", c=c)
        jobs = [(wq, raw[0][:, :, :], 1.0), (wk, raw[1][:, :, :], 1.0), (wv, raw[2][:, :, :], 1.0),
                (wo, raw[3][:, :, :], gates[:, 1:2])]
        turned_jobs = [((protoT[0][:, :, :], protoT[1][:, :, :]), cols(0, DC, NPROTO), 1.0)]
        for c in range(DC):
            turned_jobs.append(((downT[0][:, c, :], downT[1][:, c, :]), psum[:, (1 + c) * BANK:(2 + c) * BANK], 1.0))
        for c in range(LC // 2):
            turned_jobs.append(((upT[0][:, 2 * c:2 * c + 2, :], upT[1][:, 2 * c:2 * c + 2, :]), cols(3 + c, 2, D),
                                gates[:, 3:4]))

        @block.sync
        def _(sp):
            sp.dma_start(raw_p[:, :], protos).then_inc(raw_in[4], 16)
            sp.dma_start(raw_b[:, :, :], low_b.rearrange("n r d -> (n r) d").rearrange("(c p) d -> p c d", p=P))\
                .then_inc(raw_in[5], 16)
            for n, w in enumerate((w_q, w_k, w_v)):
                sp.dma_start(raw[n][:, :, :], w.rearrange("(c p) h k -> p c (h k)", p=P)).then_inc(raw_in[n], 16)
            sp.dma_start(raw[3][:, :, :], w_o.rearrange("h k d -> (h k) d").rearrange("(b p) d -> p b d", p=P))\
                .then_inc(raw_in[3], 16)
            sp.dma_start(bias0_row[:, :], row(bias0, P, D)).then_inc(small_in, 16)
            sp.dma_start(mit[:, :], row(temp, P, 1)).then_inc(small_in, 16)
            sp.wait_ge(bias_zero, 1)
            sp.dma_start(low_bias_sb[0:NPROTO, :], low_bias).then_inc(small_in, 16)

        @block.gpsimd
        def _(pool):
            pool.memset(low_bias_sb[:, :], 0.0).then_inc(bias_zero, 1)
            pool.memset(ones[:, :], 1.0).then_inc(ones_set, 1)
            with nc.allow_non_contiguous_dma("second low-rank factors, RANK values at a time"):
                for a in range(DC):
                    pool.dma_start(raw_a[:, a, :].rearrange("p (n r) -> p n r", n=NPROTO),
                                   low_a.rearrange("n (a p) r -> a p n r", p=P)[a]).then_inc(raw_in[6], 16)

        @block.tensor
        def _(pe):
            pe.wait_ge(raw_in[4], 16)
            for c in range(DC):
                last = nc.tensor.transpose(cols(0, DC, NPROTO)[:, c, :], raw_p[:, c * P:(c + 1) * P],
                                           ident[0:NPROTO, 0:NPROTO])
            last.then_inc(turned, 1)
            pe.wait_ge(raw_in[5], 16)
            for c in range(DC):
                for b in range(LC):
                    last = nc.tensor.transpose(psum[:, (1 + c) * BANK + b * P:(1 + c) * BANK + (b + 1) * P],
                                               raw_b[:, b, c * P:(c + 1) * P], ident[:, :])
                last.then_inc(turned, 1)
            pe.wait_ge(raw_in[6], 16 * DC)
            for c in range(LC // 2):
                for b in range(2):
                    for a in range(DC):
                        last = nc.tensor.transpose(cols(3 + c, 2, D)[:, b, a * P:(a + 1) * P],
                                                   raw_a[:, a, (2 * c + b) * P:(2 * c + b + 1) * P], ident[:, :])
                last.then_inc(turned, 1)
            pe.wait_ge(sq_done, 1)
            pe.wait_ge(ones_set, 1)
            for c in range(DC):
                last = nc.tensor.matmul(psum[:, 5 * BANK:5 * BANK + NPROTO], ones[:, :], sq[:, c, :], start=c == 0,
                                        stop=c == DC - 1)
            last.then_inc(sq_full, 1)

        @block.scalar
        def _(act):
            act.wait_ge(turned, 1)
            act.activation(sq[:, :, :], cols(0, DC, NPROTO), ACT.Square).then_inc(sq_done, 1)
            for n, (parts, src, scale) in enumerate(turned_jobs):
                act.wait_ge(turned, n + 1)
                split(nc, True, *parts, src, scale, hi_done, n + 1, lo_done)
            for n, (parts, src, scale) in enumerate(jobs):
                act.wait_ge(raw_in[n], 16)
                split(nc, True, parts[0][:, :, :], parts[1][:, :, :], src, scale, hi_done, 0, lo_done)

        @block.vector
        def _(dve):
            for n, (parts, src, scale) in enumerate(turned_jobs):
                split(nc, False, *parts, src, scale, hi_done, n + 1, lo_done)
            for n, (parts, src, scale) in enumerate(jobs):
                split(nc, False, parts[0][:, :, :], parts[1][:, :, :], src, scale, hi_done,
                      len(turned_jobs) + n + 1, lo_done)
            dve.wait_ge(sq_full, 1)
            nc.vector.tensor_copy(proto_sq[:, :], psum[:, 5 * BANK:5 * BANK + NPROTO])
            dve.wait_ge(small_in, 48)
            nc.vector.tensor_scalar(low_bias_sb[:, :], low_bias_sb[:, :], gates[:, 3:4], None, ALU.mult)
            nc.vector.tensor_scalar(bias0_row[:, :], bias0_row[:, :], gates[:, 2:3], None, ALU.mult)
            step = Steps(dve, step_sem, 0, 4)
            step(nc.vector.tensor_scalar(neg[:, :], mit[:, :], -1.0, None, ALU.mult))
            step(nc.vector.tensor_tensor(mit[:, :], mit[:, :], neg[:, :], ALU.max))
            step(nc.vector.tensor_scalar(mit[:, :], mit[:, :], 0.1, -1.0, ALU.max, ALU.mult))
            nc.vector.reciprocal(mit[:, :], mit[:, :])
    ffn = {"down": downT, "up": upT, "protoT": protoT, "bias": low_bias_sb, "proto_sq": proto_sq,
           "minus_inv_temp": mit}
    return (wq, wk, wv, wo), bias0_row, ffn


def expert_phase(nc, ctx, psum, const, x1, weights, indices, w1, w2):
    GT = 2 * P
    G = MOE_T // GT
    TG = GT // P
    HN = G * FC
    YN = MOE_TILES
    BANKS = 4
    ident, eps, iota, gates = const["ident"], const["eps"], const["iota"], const["gates"]
    sb = lambda n, s, d=FP32: ctx.enter_context(nc.sbuf_tensor(f"moe_{n}", s, d))
    sem = lambda n: ctx.enter_context(nc.semaphore(f"moe_{n}"))
    pair = lambda n, s: (sb(n + "_hi", s, F32R), sb(n + "_lo", s, F32R))
    xm = sb("x", [P, MOE_TILES, D])
    xn = [sb(f"xn{p}", [P, D]) for p in range(2)]
    xnT = pair("xnT", [P, DC, MOE_T])
    raw1 = [sb(f"raw1_{p}", [P, DC * FF]) for p in range(2)]
    raw2 = [sb(f"raw2_{p}", [P, FC * D]) for p in range(2)]
    w1s = [pair(f"w1_{p}", [P, DC * FF]) for p in range(2)]
    w2s = [pair(f"w2_{p}", [P, FC * D]) for p in range(2)]
    hid = [sb(f"hid{p}", [P, GT]) for p in range(2)]
    hidT = [pair(f"hidT{p}", [P, FC, GT]) for p in range(2)]
    idx, idxf, wts = sb("idx", [P, MOE_TILES, TOPK], I32), sb("idxf", [P, MOE_TILES * TOPK]), sb("wts", [P, MOE_TILES * TOPK])
    choice, comb = sb("choice", [P, MOE_TILES * TOPK, E]), sb("comb", [P, MOE_TILES, E])
    stats, mv = sb("stats", [P, MOE_TILES, 6]), sb("mv", [P, MOE_TILES, 2])
    lnv, rstd, nwt = sb("lnv", [P, MOE_TILES]), sb("rstd", [P, MOE_TILES]), sb("nwt", [P, MOE_TILES])
    hbank = [psum[:, n * BANK:n * BANK + GT] for n in range(BANKS)]
    ybank = [psum[:, (BANKS + n) * BANK:(BANKS + n) * BANK + D] for n in range(BANKS)]
    CH = DC * FF // (HN // 2)

    x_in, route_in, out_done = sem("x_in"), sem("route_in"), sem("out_done")
    w_in = [sem(f"w_in{p}") for p in range(2)]
    chain, ln_stats, ln_log, ln_rough = sem("chain"), sem("ln_stats"), sem("ln_log"), sem("ln_rough")
    xn_ready, xnT_full, xnT_hi, xnT_ready = sem("xn_ready"), sem("xnT_full"), sem("xnT_hi"), sem("xnT_ready")
    wsplit_hi, wsplit = sem("wsplit_hi"), sem("wsplit")
    h_full, gelu_done, hid_hi, hid_ready = sem("h_full"), sem("gelu_done"), sem("hid_hi"), sem("hid_ready")
    y_full, y_added = sem("y_full"), sem("y_added")

    def experts(eng, body):
        with eng.Fori(0, E // 2 - 1) as j:
            for p in range(2):
                body(j * 2 + p, p)
        for p in range(2):
            body(E - 2 + p, p)

    rows = x1.rearrange("b (j p) d -> p (b j) d", p=P)[:, 0:MOE_TILES, :]
    block = ctx.enter_context(nc.Block())

    @block.sync
    def _(sp):
        sp.dma_start(xm[:, :, :], rows).then_inc(x_in, 16)
        sp.dma_start(idx[:, :, :], indices.rearrange("(t p) k -> p t k", p=P)).then_inc(route_in, 16)
        sp.dma_start(wts[:, :].rearrange("p (t k) -> p t k", k=TOPK), weights.rearrange("(t p) k -> p t k", p=P))\
            .then_inc(route_in, 16)
        for e in range(E):
            if e >= 2:
                sp.wait_ge(wsplit, (e - 1) * HN)
            sp.dma_start(raw1[e % 2][:, :].rearrange("p (c f) -> p c f", c=DC),
                         w1[e].rearrange("(c p) f -> p c f", p=P)).then_inc(w_in[e % 2], 16)
            sp.dma_start(raw2[e % 2][:, :].rearrange("p (c d) -> p c d", c=FC),
                         w2[e].rearrange("(c p) d -> p c d", p=P)).then_inc(w_in[e % 2], 16)
        for t in range(MOE_TILES):
            sp.wait_ge(y_added, (E - 1) * YN + t + 1)
            sp.dma_start(rows[:, t, :], xm[:, t, :]).then_inc(out_done, 16)
        sp.wait_ge(out_done, 16 * MOE_TILES)

    @block.scalar
    def _(act):
        load_ln_exp_tables(nc)
        act.wait_ge(ln_stats, 1)
        act.activation(lnv[:, :], mv[:, :, 1], ACT.Ln, bias=eps[:, 0:1]).then_inc(ln_log, 1)
        act.wait_ge(ln_log, 1)
        act.activation(rstd[:, :], lnv[:, :], ACT.Exp, scale=-0.5).then_inc(ln_rough, 1)
        for t in range(MOE_TILES):
            act.wait_ge(xnT_full, t + 1)
            act.activation(xnT[0][:, :, t * P:(t + 1) * P], hbank[t % BANKS].rearrange("p (c s) -> p c s", c=DC),
                           ACT.Copy).then_inc(xnT_hi, 1)

        def body(e, p):
            for n in range(HN):
                g, m, at = n // FC, n % FC, e * HN + n
                act.wait_ge(h_full, at + 1)
                need(act, hid_ready, at - 1)
                act.activation(hid[n % 2][:, :], hbank[n % BANKS], ACT.Gelu).then_inc(gelu_done, 1)
                act.wait_ge(gelu_done, at + 1)
                act.activation(hidT[g % 2][0][:, m, :], hid[n % 2][:, :], ACT.Copy).then_inc(hid_hi, 1)

        def first(e, p):
            body(e, p)

        for p in range(2):
            first(p, p)
        with act.Fori(1, E // 2) as j:
            for p in range(2):
                body(j * 2 + p, p)

    @block.tensor
    def _(pe):
        for t in range(MOE_TILES):
            pe.wait_ge(xn_ready, t + 1)
            if t >= BANKS:
                pe.wait_ge(xnT_ready, t - BANKS + 1)
            for c in range(DC):
                last = nc.tensor.transpose(hbank[t % BANKS][:, c * P:(c + 1) * P], xn[t % 2][:, c * P:(c + 1) * P],
                                           ident[:, :])
            last.then_inc(xnT_full, 1)
        pe.wait_ge(xnT_ready, MOE_TILES)

        def hidden(e, p, g):
            for m in range(FC):
                n = g * FC + m
                need(pe, gelu_done, e * HN + n + 1 - BANKS)
                for c in range(DC):
                    at = c * FF + m * P
                    last = matmul3(nc, hbank[n % BANKS], [w[:, at:at + P] for w in w1s[p]],
                                   [a[:, c, g * GT:(g + 1) * GT] for a in xnT], c == 0, c == DC - 1)
                last.then_inc(h_full, 1)

        def outputs(e, p, g):
            need(pe, hid_ready, e * HN + (g + 1) * FC)
            for a in range(TG):
                n = g * TG + a
                need(pe, y_added, e * YN + n + 1 - BANKS)
                for m in range(FC):
                    last = matmul3(nc, ybank[n % BANKS], [x[:, m, a * P:(a + 1) * P] for x in hidT[g % 2]],
                                   [w[:, m * D:(m + 1) * D] for w in w2s[p]], m == 0, m == FC - 1)
                last.then_inc(y_full, 1)

        def body(e, p):
            need(pe, wsplit, (e + 1) * HN)
            for g in range(G):
                hidden(e, p, g)
                if g > 0:
                    outputs(e, p, g - 1)
            outputs(e, p, G - 1)

        for p in range(2):
            body(p, p)
        with pe.Fori(1, E // 2) as j:
            for p in range(2):
                body(j * 2 + p, p)

    @block.vector
    def _(dve):
        dve.wait_ge(x_in, 16)
        step = Steps(dve, chain, 0, 10)
        for t in range(MOE_TILES):
            last = nc.vector.bn_stats(stats[:, t, :], xm[:, t, :])
        step(last)
        for t in range(MOE_TILES):
            last = nc.vector.bn_aggr(mv[:, t, :], stats[:, t, :])
        last.then_inc(ln_stats, 1)
        dve.wait_ge(route_in, 32)
        step(nc.vector.tensor_copy(idxf[:, :], idx[:, :, :].rearrange("p t k -> p (t k)")))
        step(nc.vector.tensor_scalar(wts[:, :], wts[:, :], gates[:, 2:3], None, ALU.mult))
        n = MOE_TILES * TOPK
        step(nc.vector.tensor_tensor(choice[:, :, :], idxf[:, :].unsqueeze(2).broadcast_to([P, n, E]),
                                     iota[:, 0:E].unsqueeze(1).broadcast_to([P, n, E]), ALU.is_equal))
        step(nc.vector.tensor_tensor(choice[:, :, :], choice[:, :, :], wts[:, :].unsqueeze(2).broadcast_to([P, n, E]),
                                     ALU.mult))
        both = choice[:, :, :].rearrange("p (t k) e -> p t k e", k=TOPK)
        step(nc.vector.tensor_tensor(comb[:, :, :], both[:, :, 0, :], both[:, :, 1, :], ALU.add))
        dve.wait_ge(ln_stats, 1)
        dve.wait_ge(ln_rough, 1)
        step(nc.vector.tensor_tensor(nwt[:, :], rstd[:, :], rstd[:, :], ALU.mult))
        step(nc.vector.scalar_tensor_tensor(out=nwt[:, :], in0=mv[:, :, 1], scalar=EPS, in1=nwt[:, :], op0=ALU.add,
                                            op1=ALU.mult))
        step(nc.vector.tensor_scalar(nwt[:, :], nwt[:, :], -0.5, 1.5, ALU.mult, ALU.add))
        step(nc.vector.tensor_tensor(rstd[:, :], rstd[:, :], nwt[:, :], ALU.mult))

        def normed_lo(t):
            dve.wait_ge(xnT_hi, t + 1)
            nc.vector.tensor_tensor(xnT[1][:, :, t * P:(t + 1) * P], hbank[t % BANKS].rearrange("p (c s) -> p c s", c=DC),
                                    plain(xnT[0][:, :, t * P:(t + 1) * P]), ALU.subtract).then_inc(xnT_ready, 1)

        for t in range(MOE_TILES):
            if t >= 2:
                normed_lo(t - 2)
            nc.vector.tensor_scalar(xn[t % 2][:, :], xm[:, t, :], mv[:, t, 0:1], rstd[:, t:t + 1], ALU.subtract,
                                    ALU.mult).then_inc(xn_ready, 1)
        for t in range(MOE_TILES - 2, MOE_TILES):
            normed_lo(t)

        def split_weights(e, p, n):
            raw, parts = (raw1[p], w1s[p]) if n < HN // 2 else (raw2[p], w2s[p])
            at = n % (HN // 2) * CH
            cols = slice(at, at + CH)
            nc.vector.tensor_copy(parts[0][:, cols], raw[:, cols]).then_inc(wsplit_hi, 1)
            dve.wait_ge(wsplit_hi, e * HN + n + 1)
            nc.vector.tensor_tensor(parts[1][:, cols], raw[:, cols], plain(parts[0][:, cols]), ALU.subtract)\
                .then_inc(wsplit, 1)

        def add_outputs(e, g):
            for a in range(TG):
                t = g * TG + a
                need(dve, y_full, e * YN + t + 1)
                need(dve, y_added, (e - 1) * YN + t + 1)
                nc.vector.scalar_tensor_tensor(out=xm[:, t, :], in0=ybank[t % BANKS], scalar=comb_at(t, e),
                                               in1=xm[:, t, :], op0=ALU.mult, op1=ALU.add).then_inc(y_added, 1)

        def comb_at(t, e):
            return comb[:, t, bass.ds(e, 1)]

        def body(e, p, ahead):
            if ahead:
                need(dve, y_full, e * YN)
                dve.wait_ge(w_in[1 - p], ((e + 1 - (1 - p)) // 2 + 1) * 32 if isinstance(e, int) else turn[0])
            for n in range(HN):
                g, m = n // FC, n % FC
                dve.wait_ge(hid_hi, e * HN + n + 1)
                nc.vector.tensor_tensor(hidT[g % 2][1][:, m, :], hid[n % 2][:, :], plain(hidT[g % 2][0][:, m, :]),
                                        ALU.subtract).then_inc(hid_ready, 1)
                if ahead:
                    split_weights(e + 1, 1 - p, n)
                if m == FC - 2 and g > 0:
                    add_outputs(e, g - 1)
            add_outputs(e, G - 1)

        turn = [None]
        dve.wait_ge(w_in[0], 32)
        for n in range(HN):
            split_weights(0, 0, n)
        for p in range(2):
            body(p, p, True)
        with dve.Fori(1, E // 2 - 1) as j:
            for p in range(2):
                turn[0] = (j + p) * 32 + 32
                body(j * 2 + p, p, True)
        for p in range(2):
            body(E - 2 + p, p, p == 0)


def flamingo_layers(nc, ins, out):
    x1 = nc.dram_tensor("x1", (NB, SEQ, D), FP32).ap()
    batches = lambda a: a.rearrange("b (j p) d -> b p j d", p=P)
    tiles = lambda a: a.rearrange("b (j p) d -> (b j) p d", p=P)
    with ExitStack() as ctx:
        psum = ctx.enter_context(nc.psum_tensor("banks", [P, 8 * BANK], FP32))[:, :]
        const = constants(nc, ctx, ins["g_xattn"], ins["g_ffn"])
        with ExitStack() as layer:
            w, q_scale, bq, bk, bv, bo = layer0_weights(
                nc, layer, psum, const, *(ins[f"L0_xattn_{k}_{n}"] for n in "qkvo" for k in "wb"))
            attention_phase(nc, layer, psum, const, "a0", batches(ins["x"]), tiles(x1), ins["ctx_1024"], D // H, w,
                            q_scale, bq, bk, bv, bo, False, None)
        with ExitStack() as layer:
            expert_phase(nc, layer, psum, const, x1, ins["L0_ffn_expert_weights"], ins["L0_ffn_expert_indices"],
                         ins["L0_ffn_w1"], ins["L0_ffn_w2"])
        with ExitStack() as layer:
            w, bias0, ffn = layer1_weights(
                nc, layer, psum, const, *(ins[f"L1_xattn_W{n}"] for n in "qkvo"), ins["L1_ffn_prototypes"],
                ins["L1_ffn_B"], ins["L1_ffn_A"], ins["L1_ffn_bias"], ins["L1_ffn_temp"], ins["L0_ffn_bias"])
            attention_phase(nc, layer, psum, const, "a1", batches(x1), tiles(out), ins["ctx_1024"], 64, w,
                            64.0 ** -0.5, None, None, None, bias0, True, ffn)


_INS = ["x", "ctx_1024", "g_xattn", "g_ffn", "L0_xattn_w_q", "L0_xattn_b_q", "L0_xattn_w_k", "L0_xattn_b_k",
        "L0_xattn_w_v", "L0_xattn_b_v", "L0_xattn_w_o", "L0_xattn_b_o", "L0_ffn_expert_weights",
        "L0_ffn_expert_indices", "L0_ffn_w1", "L0_ffn_w2", "L0_ffn_bias", "L1_xattn_Wq", "L1_xattn_Wk",
        "L1_xattn_Wv", "L1_xattn_Wo", "L1_ffn_prototypes", "L1_ffn_B", "L1_ffn_A", "L1_ffn_bias", "L1_ffn_temp"]


def kernel(**inputs):
    import numpy as _np
    import concourse.bacc as _bacc
    from concourse import mybir as _mybir
    from concourse.bass_utils import run_bass_kernel_spmd as _run

    nc = _bacc.Bacc("TRN2", target_bir_lowering=False, num_devices=1)
    arrays, ins = {}, {}
    for name in _INS:
        a = _np.ascontiguousarray(inputs[name])
        a = a.reshape(a.shape or (1,))
        arrays[f"in_{name}"] = a
        ins[name] = nc.dram_tensor(f"in_{name}", a.shape, _mybir.dt.from_np(a.dtype), kind="ExternalInput").ap()
    out = nc.dram_tensor("out", (NB, SEQ, D), FP32, kind="ExternalOutput").ap()
    flamingo_layers(nc, ins, out)
    r = _run(nc, [arrays], core_ids=[0])
    return r.results[0]["out"]
```

```python
import concourse.bass as bass
from concourse import mybir
from contextlib import ExitStack

FP32 = mybir.dt.float32
F32R = mybir.dt.float32r
F16 = mybir.dt.float16
I32 = mybir.dt.int32
U32 = mybir.dt.uint32
ALU = mybir.AluOpType
ACT = mybir.ActivationFunctionType
AX = mybir.AxisListType

P = 128
NB, SEQ, D = 64, 256, 256
DC = D // P
TPB = SEQ // P
NT = NB * TPB
KEYS = 77
H = 16
SC = H * KEYS
ROWS = NB * KEYS
KV_COLS = D + H * 64
VALUE_TOP = 16384.0
BANK = 512
WORK = 5
EPS = 1e-5
TINY = 1e-30
NPROTO, RANK = 32, 16
LOW = NPROTO * RANK
LC = LOW // P
E, TOPK, FF, MOE_T = 8, 2, 1024, 1024
FC = FF // P
MOE_TILES = MOE_T // P
LN_EXP_TABLES = 6


def need(eng, sem, value):
    if not isinstance(value, int) or value > 0:
        eng.wait_ge(sem, value)


def live(t, n):
    return not isinstance(t, int) or 0 <= t < n


class Steps:

    def __init__(self, eng, sem, turn, per):
        self.eng, self.sem, self.base, self.per, self.k = eng, sem, turn * per, per, 0

    def __call__(self, ins):
        self.k += 1
        assert self.k <= self.per
        ins.then_inc(self.sem, 1)
        self.eng.wait_ge(self.sem, self.base + self.k)


class Ring:

    def __init__(self, uses, banks, first, last, steady):
        self.banks, self.steady = banks, steady
        self.flat, self.at_use = [], {}
        for i in range(first, last):
            for name in uses(i):
                self.at_use[i, name] = len(self.flat)
                self.flat.append((i, name))
        self.per = len(uses(steady))
        assert self.per % banks == 0
        tails = [uses(i)[-banks:] for i in (steady - 1, steady)]
        assert tails[0] == tails[1]

    def fill(self, i, name):
        n = self.at_use[i if isinstance(i, int) else self.steady, name]
        k = n // self.banks + 1
        return n % self.banks, k if isinstance(i, int) else (i - self.steady) * (self.per // self.banks) + k

    def before(self, i, name):
        n = self.at_use[i if isinstance(i, int) else self.steady, name] - self.banks
        if n < 0:
            return None
        at, what = self.flat[n]
        return (at if isinstance(i, int) else i + (at - self.steady)), what


def load_ln_exp_tables(nc):
    nc.scalar.add_instruction(mybir.InstLoadActFuncSet(
        act_func_set_id=LN_EXP_TABLES, name=nc.get_next_instruction_name(),
        engine=mybir.EngineType.Activation, ins=[], outs=[]))


def matmul3(nc, out, lhs, rhs, start, stop):
    nc.tensor.matmul(out, lhs[0], rhs[0], start=start, stop=False)
    nc.tensor.matmul(out, lhs[0], rhs[1], start=False, stop=False)
    return nc.tensor.matmul(out, lhs[1], rhs[0], start=False, stop=stop)


def row(ap, parts, n):
    return ap.rearrange("(a n) -> a n", a=1).broadcast_to([parts, n])


def plain(ap):
    return ap.bitcast(FP32)


def attention_phase(nc, ctx, psum, const, name, src, dst, keys, values, head, wq, wo, q_scale, q_bias, residual_row,
                    norm_residual, ffn):
    ident, eps = const["ident"], const["eps"]
    HB = P // head
    BLK = H // HB
    QU = max(2, BLK // 2)
    QB = BLK // QU
    OU = max(1, BLK // 4)
    OB = BLK // OU
    BODIES = 4
    SLOTS = 8 if ffn else 4
    LU = 2
    AU, AH = 2, H // 2
    XU = 1 if ffn else 2
    LAG = 7 if ffn else 3
    END = NB + (LAG + TPB - 1) // TPB
    QK = KEYS // 4
    OWN = 0 if ffn else 5
    REST = H - OWN
    EXP_AT = 2 if ffn else 3
    SUM_STEPS, LN_STEPS, LN2_STEPS, GAP_STEPS = 2, 5, 7, 1

    sb = lambda n, s, d=FP32: ctx.enter_context(nc.sbuf_tensor(f"{name}_{n}", s, d))
    sem = lambda n: nc.alloc_semaphore(f"{name}_{n}")
    pair = lambda n, s: (sb(n + "_hi", s, F32R), sb(n + "_lo", s, F32R))

    x_sb = [sb(f"x{n}", [P, TPB, D]) for n in range(BODIES)]
    res = x_sb if norm_residual else [sb(f"res{n}", [P, TPB, D]) for n in range(BODIES)]
    xn = sb("xn", [P, TPB, D])
    xnT = pair("xnT", [P, DC, SEQ])
    qT = [sb(f"qT{p}", [P, BLK, SEQ]) for p in range(2)]
    kbd = [sb(f"kbd{p}", [P, BLK, HB, KEYS]) for p in range(2)]
    v_sb = [sb(f"v{p}", [KEYS, 2, H * head], F16) for p in range(2)]
    prob = [sb(f"prob{p}", [P, SC]) for p in range(2)]
    probT = [sb(f"probT_{n}", [KEYS, H, P], F16) for n in ("hi", "lo")]
    smax, rsum, minus_max = sb("smax", [P, H]), sb("rsum", [P, H]), sb("minus_max", [P, max(1, OWN)])
    half = sb("half", [P, H, 2 * QK])
    quarter = [sb(f"quarter{p}", [P, H, QK]) for p in range(2)]
    att = sb("att", [P, H * head])
    attT = pair("attT", [P, BLK, P])
    y_sb = [sb(f"y{s}", [P, D]) for s in range(SLOTS)]
    stats, mv = sb("stats", [P, TPB, 6]), sb("mv", [P, TPB, 2])
    lnv, rstd, nwt, vare = (sb(n, [P, TPB]) for n in ("lnv", "rstd", "nwt", "vare"))
    idle, numbers = sb("idle", [P, 1]), sb("numbers", [P, 4])
    if ffn:
        stats2, mv2 = sb("stats2", [P, 6]), sb("mv2", [P, 2])
        lnv2, rstd2, nwt2, vare2 = (sb(n, [P, 1]) for n in ("lnv2", "rstd2", "nwt2", "vare2"))
        yn = sb("yn", [P, D])
        ynT = pair("ynT", [P, DC, P])
        ysq = sb("ysq", [P, TPB])
        dots, near = sb("dots", [P, NPROTO]), sb("near", [P, NPROTO])
        top, topi, topf = sb("top", [P, 8]), sb("topi", [P, 8], U32), sb("topf", [P, 2])
        lnd, rdist, dist = sb("lnd", [P, 2]), sb("rdist", [P, 2]), sb("dist", [P, 2])
        dsum, dgap, late, wtop = sb("dsum", [P, 1]), sb("dgap", [P, 1]), sb("late", [P, 1]), sb("wtop", [P, 2])
        pick = sb("pick", [P, 2, NPROTO])
        wsel = sb("wsel", [P, P])
        wselT = sb("wselT", [P, P])
        low = [sb(f"low{p}", [P, LOW]) for p in range(2)]
        hw = sb("hw", [P, LOW])
        hwT = pair("hwT", [P, LC, P])

    ps_scores = psum[:, 0:3 * BANK]
    work = [psum[:, (3 + s) * BANK:(4 + s) * BANK] for s in range(WORK)]

    x_in = [sem(f"x_in{n}") for n in range(BODIES)]
    kbd_in = [sem(f"kbd_in{p}") for p in range(2)]
    v_in = [sem(f"v_in{p}") for p in range(2)]
    out_done = [sem(f"out_done{s}") for s in range(SLOTS)]
    work_full = [sem(f"work_full{s}") for s in range(WORK)]
    kbd_zero, wsel_zero, numbers_set, res_ready = sem("kbd_zero"), sem("wsel_zero"), sem("numbers_set"), sem("res_ready")
    ln_sums, ln_stats, ln_log, ln_rough, ln_step, ln_done, xn_ready = (
        sem("ln_sums"), sem("ln_stats"), sem("ln_log"), sem("ln_rough"), sem("ln_step"), sem("ln_done"),
        sem("xn_ready"))
    xnT_hi, xnT_ready, q_ready = sem("xnT_hi"), sem("xnT_ready"), sem("q_ready")
    scores_full, max_done, scores_read, exp_done = (
        sem("scores_full"), sem("max_done"), sem("scores_read"), sem("exp_done"))
    minus_max_ready, own_read = sem("minus_max_ready"), sem("own_read")
    sum_step, sum_done, summed, recip_done, probT_hi = (
        sem("sum_step"), sem("sum_done"), sem("summed"), sem("recip_done"), sem("probT_hi"))
    probT_ready, att_ready = sem("probT_ready"), sem("att_ready")
    attT_hi, attT_ready, y_ready = sem("attT_hi"), sem("attT_ready"), sem("y_ready")
    if ffn:
        ln2_sums, ln2_stats, ln2_log, ln2_rough, ln2_step, ln2_done, ysq_done, yn_ready = (
            sem("ln2_sums"), sem("ln2_stats"), sem("ln2_log"), sem("ln2_rough"), sem("ln2_step"), sem("ln2_done"),
            sem("ysq_done"), sem("yn_ready"))
        ynT_hi, ynT_ready, dots_read = sem("ynT_hi"), sem("ynT_ready"), sem("dots_read")
        near_ready, top_found, topi_found, top_ready, top_log, top_rough = (
            sem("near_ready"), sem("top_found"), sem("topi_found"), sem("top_ready"), sem("top_log"),
            sem("top_rough"))
        gap_step, top_used, dsum_ready, dsum_inverse, gap_ready, late_ready, late_added, wtop_ready, wtops_ready, picked, wsel_ready = (
            sem("gap_step"), sem("top_used"), sem("dsum_ready"), sem("dsum_inverse"), sem("gap_ready"), sem("late_ready"),
            sem("late_added"), sem("wtop_ready"), sem("wtops_ready"), sem("picked"),
            sem("wsel_ready"))
        low_ready, hw_ready, hwT_hi, hwT_ready, wselT_ready, out_ready = (
            sem("low_ready"), sem("hw_ready"), sem("hwT_hi"), sem("hwT_ready"), sem("wselT_ready"), sem("out_ready"))
    last_ready = out_ready if ffn else y_ready

    def prep_uses(h, part):
        rows, q = [("xnT", n) for n in range(XU)], lambda n: [("q", n)]
        if QU == 2:
            at = {(0, 2): rows, (1, 2): q(0) + q(1)}
        else:
            at = {(0, 1): rows, (0, 2): q(0), (0, 3): q(1), (1, 0): q(2), (1, 2): q(3)}
        return at.get((h, part), [])

    def uses(i):
        if i < 0:
            return [u for h in range(2) for part in range(4) for u in prep_uses(h, part)]
        names = []
        for h in range(TPB):
            t = TPB * i + h
            prep = lambda part: prep_uses(h, part) if i + 1 < NB else []
            of = lambda lag, what: what if live(t - lag, NT) and lag <= LAG else []
            names += of(2, [("probT", h, g) for g in range(2)])
            names += prep(0)
            names += of(2, [("probT", h, g) for g in range(2, 4)])
            names += of(3, [("attT", h, n) for n in range(OU)])
            names += of(7, [("hwT", h)])
            names += prep(1)
            names += of(2, [("att", h, n) for n in range(AU)])
            names += of(3, [("out", h)])
            names += of(7, [("wselT", h)])
            names += of(5, [("low", h, n) for n in range(LU)])
            names += prep(2)
            names += of(4, [("ynT", h)])
            names += of(7, [("ffn", h)])
            names += prep(3)
        return names

    ring = Ring(uses, WORK, -1, END, BODIES)

    def freed(i, use):
        what, h, n = (use + (0, 0))[:3] if isinstance(use, tuple) else (use, 0, 0)
        t = i * TPB + h
        if what == "probT":
            return probT_ready, (t - 2) * 4 + n + 1
        if what == "attT":
            return attT_ready, (t - 3) * OU + n + 1
        if what == "q":
            return q_ready, (i + 1) * QU + h + 1
        if what == "xnT":
            return xnT_ready, (i + 1) * XU + h + 1
        if what == "att":
            return att_ready, (t - 2) * AU + n + 1
        if what == "low":
            return (low_ready, (t - 5) * LU + n + 1) if n else (dots_read, t - 4)
        if what == "out":
            return y_ready, t - 2
        if what == "ynT":
            return ynT_ready, t - 3
        return {"hwT": hwT_ready, "wselT": wselT_ready, "ffn": out_ready}[what], t - 6

    def bodies(eng, body):
        for i in range(BODIES):
            body(i, i, 0)
        with eng.Fori(1, NB // BODIES - 1) as j:
            for u in range(BODIES):
                body(j * BODIES + u, u, j)
        for i in range(NB - BODIES, END):
            body(i, i % BODIES, i // BODIES)

    def turn(u, j, of, ahead=0):
        return (u + ahead) % of, j * (BODIES // of) + (u + ahead) // of

    block = ctx.enter_context(nc.Block())

    @block.sync
    def _(sp):
        def load_x(i, u, j):
            n, _ = turn(u, j, BODIES)
            if norm_residual:
                need(sp, y_ready, (i - BODIES + 1) * TPB)
            need(sp, xn_ready, i - BODIES + 1)
            need(sp, res_ready, i - BODIES + 1)
            sp.dma_start(x_sb[n][:, :, :], src[i]).then_inc(x_in[n], 16)

        def load_keys(i, u, j):
            p, _ = turn(u, j, 2)
            need(sp, scores_full, (i - 1) * TPB)
            for a in range(HB):
                sp.dma_start(kbd[p][a * head:(a + 1) * head, :, a, :], keys(i)[a * head:(a + 1) * head])\
                    .then_inc(kbd_in[p], 16)

        def load_values(i, u, j):
            p, _ = turn(u, j, 2)
            need(sp, att_ready, (i - 1) * TPB * AU)
            sp.dma_start(v_sb[p][:, :, :], values(i)).then_inc(v_in[p], 16)

        def body(i, u, j):
            if live(i + 1, NB):
                load_keys(i + 1, *ahead(u, j, 1))
            if live(i, NB):
                load_values(i, u, j)
            for h in range(TPB):
                t = i * TPB + h - LAG
                if live(t, NT):
                    slot = (TPB * u + h - LAG) % SLOTS
                    need(sp, last_ready, t + 1)
                    sp.dma_start(dst[t], y_sb[slot][:, :]).then_inc(out_done[slot], 16)
                if h == 0 and live(i + 2, NB):
                    load_x(i + 2, *ahead(u, j, 2))

        def ahead(u, j, n):
            return (u + n) % BODIES, j + (u + n) // BODIES

        sp.wait_ge(kbd_zero, 2)
        load_x(0, 0, 0)
        load_keys(0, 0, 0)
        load_x(1, 1, 0)
        bodies(sp, body)
        for s in range(SLOTS):
            sp.wait_ge(out_done[s], 16 * (NT // SLOTS))

    @block.gpsimd
    def _(pool):
        for p in range(2):
            pool.memset(kbd[p][:, :, :, :], 0.0).then_inc(kbd_zero, 1)
        if ffn:
            pool.memset(wsel[:, :], 0.0).then_inc(wsel_zero, 1)

        def residual(i, u, j):
            n, before = turn(u, j, BODIES)
            need(pool, x_in[n], (before + 1) * 16)
            need(pool, y_ready, (i - BODIES + 1) * TPB)
            pool.tensor_tensor(res[n][:, :, :], x_sb[n][:, :, :],
                               residual_row[:, :].unsqueeze(1).broadcast_to([P, TPB, D]), ALU.add)\
                .then_inc(res_ready, 1)

        def softmax_sums(t, h):
            e = prob[h][:, :].rearrange("p (h k) -> p h k", h=H)
            need(pool, exp_done, t + 1)
            need(pool, sum_done, t)
            step = Steps(pool, sum_step, t, SUM_STEPS)
            step(pool.tensor_tensor(half[:, :, :], e[:, :, 0:2 * QK], e[:, :, 2 * QK:4 * QK], ALU.add))
            need(pool, summed, t - 1)
            step(pool.tensor_tensor(quarter[h][:, :, :], half[:, :, 0:QK], half[:, :, QK:2 * QK], ALU.add))
            pool.tensor_tensor(quarter[h][:, :, 0:KEYS - 4 * QK], quarter[h][:, :, 0:KEYS - 4 * QK], e[:, :, 4 * QK:KEYS],
                               ALU.add).then_inc(sum_done, 1)

        def refine(step, var, rough, tmp, vare_, n):
            step(pool.tensor_tensor(tmp, rough, rough, ALU.mult))
            step(pool.tensor_tensor(vare_, var, numbers[:, 0:1].broadcast_to([P, n]), ALU.add))
            step(pool.tensor_tensor(tmp, tmp, vare_, ALU.mult))
            step(pool.tensor_tensor(tmp, tmp, numbers[:, 1:2].broadcast_to([P, n]), ALU.mult))
            step(pool.tensor_tensor(tmp, tmp, numbers[:, 2:3].broadcast_to([P, n]), ALU.add))

        def refine_norm(i):
            need(pool, ln_rough, i + 1)
            refine(Steps(pool, ln_step, i, LN_STEPS), mv[:, :, 1], rstd[:, :], nwt[:, :], vare[:, :], TPB)
            pool.tensor_tensor(rstd[:, :], rstd[:, :], nwt[:, :], ALU.mult).then_inc(ln_done, 1)

        def refine_norm2(t, h):
            need(pool, ln2_rough, t + 1)
            step = Steps(pool, ln2_step, t, LN2_STEPS)
            refine(step, mv2[:, 1:2], rstd2[:, :], nwt2[:, :], vare2[:, :], 1)
            pool.tensor_tensor(rstd2[:, :], rstd2[:, :], nwt2[:, :], ALU.mult).then_inc(ln2_done, 1)
            need(pool, ln2_done, t + 1)
            step(pool.tensor_tensor(nwt2[:, :], rstd2[:, :], rstd2[:, :], ALU.mult))
            step(pool.tensor_tensor(nwt2[:, :], nwt2[:, :], mv2[:, 1:2], ALU.mult))
            need(pool, near_ready, t - 1)
            pool.tensor_tensor(ysq[:, h:h + 1], nwt2[:, :], numbers[:, 3:4], ALU.mult).then_inc(ysq_done, 1)

        def distance_sum(t):
            need(pool, top_rough, t + 1)
            need(pool, late_ready, t)
            step = Steps(pool, gap_step, t, GAP_STEPS)
            step(pool.tensor_tensor(dist[:, :], top[:, 0:2], rdist[:, :], ALU.mult))
            pool.tensor_tensor(dsum[:, :], dist[:, 0:1], dist[:, 1:2], ALU.add).then_inc(dsum_ready, 1)
            pool.tensor_tensor(dgap[:, :], top[:, 1:2], top[:, 0:1], ALU.subtract).then_inc(top_used, 1)

        def distance_gap(t):
            need(pool, dsum_inverse, t + 1)
            need(pool, top_used, t + 1)
            pool.tensor_tensor(dgap[:, :], dgap[:, :], dsum[:, :], ALU.mult).then_inc(gap_ready, 1)

        def weigh(t, h):
            need(pool, wsel_ready, t + 1)
            need(pool, low_ready, (t + 1) * LU)
            need(pool, hwT_ready, t)
            pool.tensor_tensor(hw[:, :].rearrange("p (n r) -> p n r", n=NPROTO),
                               low[h][:, :].rearrange("p (n r) -> p n r", n=NPROTO),
                               wsel[:, 0:NPROTO].unsqueeze(2).broadcast_to([P, NPROTO, RANK]), ALU.mult)\
                .then_inc(hw_ready, 1)

        def body(i, u, j):
            for h in range(TPB):
                t = i * TPB + h
                if ffn and live(t - 7, NT):
                    weigh(t - 7, 1 - h)
                if live(t - 1, NT):
                    softmax_sums(t - 1, 1 - h)
                if h == 1 and live(i + 2, NB):
                    residual(i + 2, (u + 2) % BODIES, j + (u + 2) // BODIES)
                if ffn and live(t - 4, NT):
                    refine_norm2(t - 4, h)
                if ffn and live(t - 6, NT):
                    distance_sum(t - 6)
                if ffn and live(t - 6, NT):
                    distance_gap(t - 6)
                if h == 1 and live(i + 2, NB):
                    refine_norm(i + 2)

        for k, number in enumerate((EPS, -0.5, 1.5, float(D))):
            last = pool.memset(numbers[:, k:k + 1], number)
        last.then_inc(numbers_set, 1)
        pool.wait_ge(numbers_set, 1)
        for i in range(2):
            residual(i, i, 0)
            refine_norm(i)
        bodies(pool, body)

    @block.scalar
    def _(act):
        load_ln_exp_tables(nc)

        def full(i, use):
            s, k = ring.fill(i, use)
            need(act, work_full[s], k)
            return work[s]

        def inverse_deviation(var, log, out, stats_done, log_done, rough_done, turn):
            need(act, stats_done, turn + 1)
            act.activation(log, var, ACT.Ln, bias=eps[:, 0:1]).then_inc(log_done, 1)
            need(act, log_done, turn + 1)
            act.activation(out, log, ACT.Exp, scale=-0.5).then_inc(rough_done, 1)

        def split_hi(i, use, out, cols, done):
            bank = full(i, use)
            act.activation(out, bank[:, 0:cols].rearrange("p (c s) -> p c s", c=out.shape[1]), ACT.Copy)\
                .then_inc(done, 1)

        def prepare(i, p, h, part):
            for use in prep_uses(h, part):
                if use[0] == "xnT":
                    part = slice(use[1] * DC // XU, (use[1] + 1) * DC // XU)
                    split_hi(i, use, xnT[0][:, part, :], DC // XU * SEQ, xnT_hi)
                    continue
                n = use[1]
                bank = full(i, use)[:, 0:QB * SEQ].rearrange("p (b s) -> p b s", b=QB)
                out = qT[p][:, n * QB:(n + 1) * QB, :]
                if q_bias is None:
                    last = act.activation(out, bank, ACT.Copy, scale=q_scale)
                else:
                    last = act.activation(out, bank, ACT.Identity, scale=q_scale, bias=q_bias[:, n:n + 1])
                last.then_inc(q_ready, 1)

        def normalise(i):
            inverse_deviation(mv[:, :, 1], lnv[:, :], rstd[:, :], ln_stats, ln_log, ln_rough, i)

        def own_exponentials(t, h):
            need(act, minus_max_ready, t + 1)
            need(act, scores_read, t + 1)
            need(act, sum_done, t - 1)
            for a in range(REST, H):
                at = slice(a * KEYS, (a + 1) * KEYS)
                last = act.activation(prob[h][:, at], ps_scores[:, at], ACT.Exp, bias=minus_max[:, a - REST:a - REST + 1])
                if a == H - 1:
                    last.then_inc(own_read, 1)

        def body(i, u, j):
            for h in range(TPB):
                t = i * TPB + h
                prep = lambda part: prepare(i, (u + 1) % 2, h, part) if live(i + 1, NB) else None
                for g in range(4):
                    if g == EXP_AT and live(t - 1, NT):
                        need(act, scores_read, t)
                        part = prob[1 - h][:, 0:REST * KEYS]
                        act.activation(part, part, ACT.Exp).then_inc(exp_done, 1)
                    if g == 2:
                        prep(0)
                    if live(t - 2, NT):
                        bank = full(i, ("probT", h, g))
                        act.activation(probT[0][:, 4 * g:4 * g + 4, :],
                                       bank[0:KEYS, :].rearrange("p (h s) -> p h s", h=4), ACT.Copy)\
                            .then_inc(probT_hi, 1)
                if live(t - 3, NT):
                    for n in range(OU):
                        split_hi(i, ("attT", h, n), attT[0][:, n * OB:(n + 1) * OB, :], OB * P, attT_hi)
                if ffn and live(t - 7, NT):
                    split_hi(i, ("hwT", h), hwT[0][:, :, :], LC * P, hwT_hi)
                prep(1)
                if h == 1 and live(i + 2, NB):
                    normalise(i + 2)
                if ffn and live(t - 6, NT):
                    need(act, gap_ready, t - 5)
                    act.activation(late[:, :], dgap[:, :], ACT.Exp, scale=ffn["minus_inv_temp"][:, 0:1])\
                        .then_inc(late_ready, 1)
                if ffn and live(t - 7, NT):
                    bank = full(i, ("wselT", h))
                    act.activation(wselT[:, :], bank[:, 0:P], ACT.Copy).then_inc(wselT_ready, 1)
                if ffn and live(t - 5, NT):
                    need(act, hw_ready, t - 6)
                    for n in range(LU):
                        bank = full(i, ("low", h, n))
                        part = slice(n * LOW // LU, (n + 1) * LOW // LU)
                        act.activation(low[1 - h][:, part], bank[:, 0:LOW // LU], ACT.Copy).then_inc(low_ready, 1)
                if ffn and live(t - 3, NT):
                    inverse_deviation(mv2[:, 1:2], lnv2[:, :], rstd2[:, :], ln2_stats, ln2_log, ln2_rough, t - 3)
                prep(2)
                if ffn and live(t - 4, NT):
                    split_hi(i, ("ynT", h), ynT[0][:, :, :], DC * P, ynT_hi)
                if OWN and live(t, NT):
                    own_exponentials(t, h)
                prep(3)
                if ffn and live(t - 5, NT):
                    need(act, top_found, t - 4)
                    act.activation(lnd[:, :], top[:, 0:2], ACT.Ln, scale=-1.0).then_inc(top_log, 1)
                    need(act, top_log, t - 4)
                    act.activation(rdist[:, :], lnd[:, :], ACT.Exp, scale=-0.5).then_inc(top_rough, 1)

        normalise(0)
        for h in range(2):
            for part in range(4):
                prepare(-1, 0, h, part)
        normalise(1)
        bodies(act, body)

    @block.tensor
    def _(pe):
        def bank_for(i, use):
            before = ring.before(i, use)
            if before is not None:
                need(pe, *freed(*before))
            return work[ring.fill(i, use)[0]]

        def filled(ins, i, use):
            ins.then_inc(work_full[ring.fill(i, use)[0]], 1)

        def prepare(i, p, h, part):
            for use in prep_uses(h, part):
                if use[0] == "xnT":
                    need(pe, xn_ready, i + 2)
                    bank = bank_for(i, use)
                    for c in range(DC // XU):
                        at = (use[1] * DC // XU + c) * P
                        for a in range(TPB):
                            last = nc.tensor.transpose(bank[:, c * SEQ + a * P:c * SEQ + (a + 1) * P],
                                                       xn[:, a, at:at + P], ident[:, :])
                else:
                    need(pe, xnT_ready, (i + 2) * XU)
                    bank = bank_for(i, use)
                    for b in range(QB):
                        at = (use[1] * QB + b) * P
                        for c in range(DC):
                            last = matmul3(nc, bank[:, b * SEQ:(b + 1) * SEQ], [w[:, c, at:at + P] for w in wq],
                                           [a[:, c, :] for a in xnT], c == 0, c == DC - 1)
                filled(last, i, use)

        def scores(i, t, h, u, j, part):
            p, before = turn(u, j, 2)
            need(pe, kbd_in[p], (before + 1) * 16 * HB)
            need(pe, q_ready, (i + 1) * QU)
            need(pe, scores_read, t)
            if OWN:
                need(pe, own_read, t)
            for b in range(part * BLK // 2, (part + 1) * BLK // 2):
                at, end = b * HB * KEYS, (b + 1) * HB * KEYS
                while at < end:
                    to = min(end, (at // BANK + 1) * BANK)
                    last = nc.tensor.matmul(ps_scores[:, at:to], qT[p][:, b, h * P:(h + 1) * P],
                                            kbd[p][:, b, :, :].rearrange("p a k -> p (a k)")
                                            [:, at - b * HB * KEYS:to - b * HB * KEYS], start=True, stop=True)
                    at = to
            if part == 1:
                last.then_inc(scores_full, 1)

        def attend(i, t, h, u, j):
            p, before = turn(u, j, 2, -1)
            need(pe, probT_ready, (t + 1) * 4)
            need(pe, v_in[p], (before + 1) * 16)
            for n in range(AU):
                bank = bank_for(i, ("att", h, n))
                for a in range(AH):
                    at = (n * AH + a) * head
                    last = matmul3(nc, bank[:, a * head:(a + 1) * head], [x[:, n * AH + a, :] for x in probT],
                                   [v_sb[p][:, k, at:at + head] for k in range(2)], True, True)
                filled(last, i, ("att", h, n))

        def body(i, u, j):
            for h in range(TPB):
                t = i * TPB + h
                prep = lambda part: prepare(i, (u + 1) % 2, h, part) if live(i + 1, NB) else None
                for g in range(4):
                    if g == 2:
                        prep(0)
                    if ffn and g == 3 and live(t, NT):
                        scores(i, t, h, u, j, 0)
                    if live(t - 2, NT):
                        need(pe, exp_done, t - 1)
                        bank = bank_for(i, ("probT", h, g))
                        for a in range(4):
                            at = (4 * g + a) * KEYS
                            last = nc.tensor.transpose(bank[0:KEYS, a * P:(a + 1) * P], prob[h][:, at:at + KEYS],
                                                       ident[:, :])
                        filled(last, i, ("probT", h, g))
                if live(t - 3, NT):
                    need(pe, att_ready, (t - 2) * AU)
                    for n in range(OU):
                        bank = bank_for(i, ("attT", h, n))
                        for b in range(OB):
                            at = (n * OB + b) * P
                            last = nc.tensor.transpose(bank[:, b * P:(b + 1) * P], att[:, at:at + P], ident[:, :])
                        filled(last, i, ("attT", h, n))
                if live(t, NT):
                    for part in range(1 if ffn else 0, 2):
                        scores(i, t, h, u, j, part)
                if ffn and live(t - 7, NT):
                    need(pe, hw_ready, t - 6)
                    bank = bank_for(i, ("hwT", h))
                    for c in range(LC):
                        last = nc.tensor.transpose(bank[:, c * P:(c + 1) * P], hw[:, c * P:(c + 1) * P], ident[:, :])
                    filled(last, i, ("hwT", h))
                prep(1)
                if live(t - 2, NT):
                    attend(i, t - 2, h, u, j)
                if live(t - 3, NT):
                    need(pe, attT_ready, (t - 2) * OU)
                    bank = bank_for(i, ("out", h))
                    for b in range(BLK):
                        last = matmul3(nc, bank[:, 0:D], [a[:, b, :] for a in attT], [w[:, b, :] for w in wo],
                                       b == 0, b == BLK - 1)
                    filled(last, i, ("out", h))
                if ffn and live(t - 7, NT):
                    need(pe, wsel_ready, t - 6)
                    bank = bank_for(i, ("wselT", h))
                    filled(nc.tensor.transpose(bank[:, 0:P], wsel[:, :], ident[:, :]), i, ("wselT", h))
                if ffn and live(t - 5, NT):
                    need(pe, ynT_ready, t - 4)
                    for n in range(LU):
                        bank = bank_for(i, ("low", h, n))
                        cols = LOW // LU + (NPROTO if n == 0 else 0)
                        for c in range(DC):
                            last = matmul3(nc, bank[:, 0:cols], [a[:, c, :] for a in ynT],
                                           [w[:, c, n, 0:cols] for w in ffn["down"]], c == 0, c == DC - 1)
                        filled(last, i, ("low", h, n))
                prep(2)
                if ffn and live(t - 4, NT):
                    need(pe, yn_ready, t - 3)
                    bank = bank_for(i, ("ynT", h))
                    for c in range(DC):
                        last = nc.tensor.transpose(bank[:, c * P:(c + 1) * P], yn[:, c * P:(c + 1) * P], ident[:, :])
                    filled(last, i, ("ynT", h))
                if ffn and live(t - 7, NT):
                    need(pe, hwT_ready, t - 6)
                    need(pe, wselT_ready, t - 6)
                    bank = bank_for(i, ("ffn", h))
                    for c in range(LC):
                        matmul3(nc, bank[:, 0:D], [a[:, c, :] for a in hwT], [w[:, c, :] for w in ffn["up"]],
                                c == 0, False)
                    filled(nc.tensor.matmul(bank[:, 0:D], wselT[:, :], ffn["bias"][:, :], start=False, stop=True),
                           i, ("ffn", h))
                prep(3)

        if ffn:
            pe.wait_ge(wsel_zero, 1)
        for h in range(2):
            for part in range(4):
                prepare(-1, 0, h, part)
        bodies(pe, body)

    @block.vector
    def _(dve):
        def full(i, use):
            s, k = ring.fill(i, use)
            need(dve, work_full[s], k)
            return work[s]

        def hold(sem_, value):
            need(dve, sem_, value)
            nc.vector.memset(idle[:, :], 0.0)

        def split_lo(i, use, hi, lo, cols, hi_done, turn, done):
            bank = full(i, use)
            need(dve, hi_done, turn)
            nc.vector.tensor_tensor(lo, bank[:, 0:cols].rearrange("p (c s) -> p c s", c=hi.shape[1]), plain(hi),
                                    ALU.subtract).then_inc(done, 1)

        def norm_stats(i, u, j):
            n, before = turn(u, j, BODIES)
            if norm_residual:
                need(dve, res_ready, i + 1)
            else:
                need(dve, x_in[n], (before + 1) * 16)
            for a in range(TPB):
                last = nc.vector.bn_stats(stats[:, a, :], x_sb[n][:, a, :])
            last.then_inc(ln_sums, 1)
            hold(ln_sums, i + 1)
            for a in range(TPB):
                last = nc.vector.bn_aggr(mv[:, a, :], stats[:, a, :])
            last.then_inc(ln_stats, 1)

        def norm_apply(i, u, j):
            n, _ = turn(u, j, BODIES)
            need(dve, ln_done, i + 1)
            need(dve, ln_stats, i + 1)
            need(dve, xnT_hi, i * XU)
            for a in range(TPB):
                last = nc.vector.tensor_scalar(xn[:, a, :], x_sb[n][:, a, :], mv[:, a, 0:1], rstd[:, a:a + 1],
                                               ALU.subtract, ALU.mult)
            last.then_inc(xn_ready, 1)

        scores = ps_scores[:, 0:SC].rearrange("p (h k) -> p h k", h=H)

        def maximum(t):
            need(dve, scores_full, t + 1)
            nc.vector.reduce_max(smax[:, :], scores, AX.X).then_inc(max_done, 1)

        def shift_scores(t, h):
            need(dve, max_done, t + 1)
            if OWN:
                need(dve, own_read, t)
                nc.vector.tensor_scalar(minus_max[:, :], smax[:, REST:H], -1.0, None, ALU.mult)\
                    .then_inc(minus_max_ready, 1)
            need(dve, sum_done, t - 1)
            nc.vector.tensor_tensor(prob[h][:, 0:REST * KEYS].rearrange("p (h k) -> p h k", h=REST),
                                    scores[:, 0:REST, :], smax[:, 0:REST].unsqueeze(2).broadcast_to([P, REST, KEYS]),
                                    ALU.subtract).then_inc(scores_read, 1)

        def prototype_products(i, t, h):
            bank = full(i, ("low", h, 0))
            need(dve, near_ready, t)
            need(dve, low_ready, t * LU + 1)
            nc.vector.scalar_tensor_tensor(out=dots[:, :], in0=bank[:, LOW // LU:LOW // LU + NPROTO], scalar=2.0,
                                           in1=ffn["proto_sq"][:, :], op0=ALU.mult, op1=ALU.subtract)\
                .then_inc(dots_read, 1)

        def nearest_two(t, h):
            need(dve, dots_read, t + 1)
            need(dve, ysq_done, t + 1)
            nc.vector.tensor_scalar(near[:, :], dots[:, :], ysq[:, 1 - h:2 - h], -TINY, ALU.subtract, ALU.min)\
                .then_inc(near_ready, 1)
            need(dve, top_used, t)
            hold(near_ready, t + 1)
            nc.vector.max(top[:, :], near[:, :]).then_inc(top_found, 1)

        def nearest_index(t):
            hold(top_found, t + 1)
            nc.vector.max_index(topi[:, :], top[:, :], near[:, :]).then_inc(topi_found, 1)
            need(dve, topi_found, t + 1)
            nc.vector.tensor_copy(topf[:, :], topi[:, 0:2]).then_inc(top_ready, 1)

        def split_rows(i, h, part):
            for use in prep_uses(h, part):
                if use[0] == "xnT":
                    at = slice(use[1] * DC // XU, (use[1] + 1) * DC // XU)
                    split_lo(i, use, xnT[0][:, at, :], xnT[1][:, at, :], DC // XU * SEQ, xnT_hi,
                             (i + 1) * XU + use[1] + 1, xnT_ready)

        def scale_attention(i, t, h):
            need(dve, recip_done, t + 1)
            for n in range(AU):
                bank = full(i, ("att", h, n))
                heads = slice(n * AH, (n + 1) * AH)
                nc.vector.tensor_tensor(att[:, :].rearrange("p (h k) -> p h k", h=H)[:, heads, :],
                                        bank[:, 0:AH * head].rearrange("p (h k) -> p h k", h=AH),
                                        rsum[:, heads].unsqueeze(2).broadcast_to([P, AH, head]), ALU.mult)\
                    .then_inc(att_ready, 1)

        def place(lag, u, h, j):
            n = TPB * u + h - lag
            return n % SLOTS, j * (BODIES * TPB // SLOTS) + n // SLOTS

        def add_residual(i, t, h, u, j):
            bank = full(i, ("out", h))
            slot, before = place(3, u, h, j)
            need(dve, res_ready, i - 1 + h)
            need(dve, out_done[slot], before * 16)
            nc.vector.tensor_tensor(y_sb[slot][:, :], bank[:, 0:D], res[(u - 2 + h) % BODIES][:, 1 - h, :], ALU.add)\
                .then_inc(y_ready, 1)

        def body(i, u, j):
            for h in range(TPB):
                t = i * TPB + h
                slot = lambda lag: place(lag, u, h, j)[0]
                chosen = ffn and live(t - 6, NT)
                if live(t - 2, NT):
                    need(dve, sum_done, t - 1)
                    need(dve, att_ready, (t - 2) * AU)
                    nc.vector.reduce_sum(rsum[:, :], quarter[h][:, :, :], AX.X).then_inc(summed, 1)
                for g in range(4):
                    if live(t - 2, NT):
                        bank = full(i, ("probT", h, g))
                        part = slice(4 * g, 4 * g + 4)
                        need(dve, probT_hi, (t - 2) * 4 + g + 1)
                        nc.vector.tensor_tensor(probT[1][:, part, :], bank[0:KEYS, :].rearrange("p (h s) -> p h s", h=4),
                                                probT[0][:, part, :], ALU.subtract).then_inc(probT_ready, 1)
                if live(t - 2, NT):
                    need(dve, summed, t - 1)
                    nc.vector.reciprocal(rsum[:, :], rsum[:, :]).then_inc(recip_done, 1)
                if live(t - 3, NT):
                    for n in range(OU):
                        part = slice(n * OB, (n + 1) * OB)
                        split_lo(i, ("attT", h, n), attT[0][:, part, :], attT[1][:, part, :], OB * P, attT_hi,
                                 (t - 3) * OU + n + 1, attT_ready)
                if ffn and live(t - 7, NT):
                    split_lo(i, ("hwT", h), hwT[0][:, :, :], hwT[1][:, :, :], LC * P, hwT_hi, t - 6, hwT_ready)
                if live(i + 1, NB):
                    split_rows(i, h, 1)
                if ffn and live(t - 2, NT):
                    scale_attention(i, t - 2, h)
                if h == 1 and live(i + 2, NB):
                    norm_stats(i + 2, (u + 2) % BODIES, j + (u + 2) // BODIES)
                if chosen:
                    need(dve, dsum_ready, t - 5)
                    nc.vector.reciprocal(dsum[:, :], dsum[:, :]).then_inc(dsum_inverse, 1)
                if live(t, NT):
                    maximum(t)
                if ffn and live(t - 4, NT):
                    need(dve, ln2_done, t - 3)
                    need(dve, ynT_hi, t - 4)
                    nc.vector.tensor_scalar(yn[:, :], y_sb[slot(4)][:, :], mv2[:, 0:1], rstd2[:, 0:1],
                                            ALU.subtract, ALU.mult).then_inc(yn_ready, 1)
                if ffn and live(t - 3, NT):
                    add_residual(i, t - 3, h, u, j)
                if live(t, NT):
                    shift_scores(t, h)
                if not ffn and live(t - 2, NT):
                    scale_attention(i, t - 2, h)
                if h == 1 and live(i + 2, NB):
                    norm_apply(i + 2, (u + 2) % BODIES, j + (u + 2) // BODIES)
                if not ffn and live(t - 3, NT):
                    add_residual(i, t - 3, h, u, j)
                if live(i + 1, NB):
                    split_rows(i, h, 2)
                if chosen:
                    need(dve, late_ready, t - 5)
                    nc.vector.tensor_scalar(wtop[:, 0:1], late[:, :], 1.0, None, ALU.add).then_inc(late_added, 1)
                if ffn and live(t - 3, NT):
                    need(dve, y_ready, t - 2)
                    nc.vector.bn_stats(stats2[:, :], y_sb[slot(3)][:, :]).then_inc(ln2_sums, 1)
                if chosen:
                    need(dve, late_added, t - 5)
                    nc.vector.reciprocal(wtop[:, 0:1], wtop[:, 0:1]).then_inc(wtop_ready, 1)
                if ffn and live(t - 5, NT):
                    prototype_products(i, t - 5, h)
                if ffn and live(t - 3, NT):
                    need(dve, yn_ready, t - 3)
                    need(dve, ysq_done, t - 3)
                    hold(ln2_sums, t - 2)
                    nc.vector.bn_aggr(mv2[:, :], stats2[:, :]).then_inc(ln2_stats, 1)
                if chosen:
                    need(dve, wtop_ready, t - 5)
                    nc.vector.tensor_tensor(wtop[:, 1:2], late[:, :], wtop[:, 0:1], ALU.mult).then_inc(wtops_ready, 1)
                if chosen:
                    need(dve, wtops_ready, t - 5)
                    need(dve, top_ready, t - 5)
                    for k in range(2):
                        last = nc.vector.tensor_scalar(pick[:, k, :], const["iota"][:, :], topf[:, k:k + 1],
                                                       wtop[:, k:k + 1], ALU.is_equal, ALU.mult)
                    last.then_inc(picked, 1)
                if ffn and live(t - 4, NT):
                    split_lo(i, ("ynT", h), ynT[0][:, :, :], ynT[1][:, :, :], DC * P, ynT_hi, t - 3, ynT_ready)
                if chosen:
                    need(dve, picked, t - 5)
                    need(dve, wselT_ready, t - 6)
                    need(dve, hw_ready, t - 6)
                    nc.vector.tensor_tensor(wsel[:, 0:NPROTO], pick[:, 0, :], pick[:, 1, :], ALU.add)\
                        .then_inc(wsel_ready, 1)
                if ffn and live(t - 5, NT):
                    nearest_two(t - 5, h)
                    nearest_index(t - 5)
                if ffn and live(t - 7, NT):
                    bank = full(i, ("ffn", h))
                    y7 = y_sb[slot(7)]
                    nc.vector.tensor_tensor(y7[:, :], bank[:, 0:D], y7[:, :], ALU.add).then_inc(out_ready, 1)

        if ffn:
            dve.wait_ge(wsel_zero, 1)
        norm_stats(0, 0, 0)
        norm_apply(0, 0, 0)
        for part in range(4):
            split_rows(-1, 0, part)
        norm_stats(1, 1, 0)
        norm_apply(1, 1, 0)
        bodies(dve, body)


def split(nc, act, hi, lo, src, scale, hi_done, turn, lo_done):
    if act:
        func = ACT.Copy if isinstance(scale, float) else ACT.Identity
        nc.scalar.activation(hi, src, func, scale=scale).then_inc(hi_done, 1)
    else:
        nc.vector.wait_ge(hi_done, turn)
        nc.vector.scalar_tensor_tensor(out=lo, in0=src, scalar=scale, in1=plain(hi), op0=ALU.mult,
                                       op1=ALU.subtract).then_inc(lo_done, 1)


def constants(nc, ctx, g_xattn, g_ffn):
    sb = lambda n, s, d=FP32: ctx.enter_context(nc.sbuf_tensor(n, s, d))
    sem = lambda n: nc.alloc_semaphore(n)
    ident, iota, eps, gates = sb("ident", [P, P]), sb("iota", [P, NPROTO]), sb("eps", [P, 1]), sb("gates", [P, 4])
    out_scale = sb("out_scale", [P, 2])
    ident_zero, gates_in = sem("ident_zero"), sem("gates_in")
    with nc.Block() as block:
        @block.sync
        def _(sp):
            sp.dma_start(gates[:, 0:2], row(g_xattn, P, 2)).then_inc(gates_in, 16)
            sp.dma_start(gates[:, 2:4], row(g_ffn, P, 2)).then_inc(gates_in, 16)

        @block.gpsimd
        def _(pool):
            pool.memset(ident[:, :], 0.0).then_inc(ident_zero, 1)
            pool.memset(eps[:, :], EPS)
            pool.wait_ge(ident_zero, 1)
            pool.affine_select(out=ident[:, :], in_=ident[:, :], compare_op=ALU.not_equal, fill=1.0, base=0,
                               pattern=[[-1, P]], channel_multiplier=1)
            pool.iota(iota[:, :], [[1, NPROTO]], base=0, channel_multiplier=0, allow_small_or_imprecise_dtypes=True)

        @block.scalar
        def _(act):
            act.wait_ge(gates_in, 32)
            act.activation(gates[:, :], gates[:, :], ACT.Tanh)
    return {"ident": ident, "iota": iota, "eps": eps, "gates": gates, "out_scale": out_scale}


def keys_values_phase(nc, ctx, psum, const, context, w_k, b_k, w_v, b_v, w_k1, w_v1, kt, v):
    sb = lambda n, s, d=FP32: ctx.enter_context(nc.sbuf_tensor(f"kv_{n}", s, d))
    sem = lambda n: nc.alloc_semaphore(f"kv_{n}")
    pair = lambda n, s: (sb(n + "_hi", s, F32R), sb(n + "_lo", s, F32R))
    gates, ident, out_scale = const["gates"], const["ident"], const["out_scale"]
    W1 = H * 64
    TILES = (ROWS + P - 1) // P
    FULL = ROWS // P
    wk, wv, wk1, wv1 = pair("wk", [P, DC, D]), pair("wv", [P, DC, D]), pair("wk1", [P, DC, W1]), pair("wv1", [P, DC, W1])
    bk, bv = sb("bk", [P, DC]), sb("bv", [P, D])

    raw_in = [sem(f"raw_in{n}") for n in range(4)]
    PARTS = 4
    cut = [FULL * n // PARTS for n in range(PARTS + 1)]
    ctx_in = [sem(f"ctx_in{n}") for n in range(PARTS)]
    bias_in, turned, hi_done, lo_done = sem("bias_in"), sem("turned"), sem("hi_done"), sem("lo_done")
    parts_done = sem("parts_done")
    ones_set, abs_done, sums_full, step_sem, scale_ready = (
        sem("ones_set"), sem("abs_done"), sem("sums_full"), sem("step"), sem("scale_ready"))
    with ExitStack() as inner:
        tmp = lambda n, s: inner.enter_context(nc.sbuf_tensor(f"kv_{n}", s, FP32))
        raw = [tmp(f"raw{n}", [P, DC, D if n < 2 else W1]) for n in range(4)]
        rows = tmp("rows", [P, TILES, D])
        abs0, abs1, ones = tmp("abs0", [P, DC, D]), tmp("abs1", [P, DC, W1]), tmp("ones", [P, P])
        part_max = tmp("part_max", [P, PARTS])
        largest, bound, vscale = tmp("largest", [P, 1]), tmp("bound", [P, 2]), tmp("vscale", [P, 2])
        bias_max, v_unit = tmp("bias_max", [P, 1]), tmp("v_unit", [P, 2])
        block = inner.enter_context(nc.Block())
        bank = lambda n: psum[:, n * BANK:(n + 1) * BANK].rearrange("p (c o) -> p c o", c=DC)
        jobs = [(wk, bank(0), 1.0), (wk1, raw[2][:, :, :], 1.0), (wv, bank(1), vscale[:, 0:1]),
                (wv1, raw[3][:, :, :], vscale[:, 1:2])]

        @block.sync
        def _(sp):
            for n, w in enumerate((w_k, w_v)):
                sp.dma_start(raw[n][:, :, :], w.rearrange("(a p) d -> p a d", p=P)).then_inc(raw_in[n], 16)
            for n, w in ((3, w_v1), (2, w_k1)):
                sp.dma_start(raw[n][:, :, :], w.rearrange("(c p) h k -> p c (h k)", p=P)).then_inc(raw_in[n], 16)
            sp.dma_start(rows[0:ROWS - FULL * P, FULL, :], context[FULL * P:ROWS]).then_inc(ctx_in[PARTS - 1], 16)
            for n in range(PARTS):
                sp.dma_start(rows[:, cut[n]:cut[n + 1], :],
                             context[cut[n] * P:cut[n + 1] * P].rearrange("(t p) d -> p t d", p=P)).then_inc(ctx_in[n], 16)
            with nc.allow_non_contiguous_dma("biases, one value per partition"):
                sp.dma_start(bk[:, :], b_k.rearrange("(c p) -> p c", p=P)).then_inc(bias_in, 16)
            sp.dma_start(bv[:, :], row(b_v, P, D)).then_inc(bias_in, 16)

        @block.gpsimd
        def _(pool):
            pool.memset(ones[:, :], 1.0).then_inc(ones_set, 1)
            pool.wait_ge(ones_set, 1)
            pool.memset(rows[ROWS - FULL * P:P, FULL, :], 0.0).then_inc(ones_set, 1)

        @block.tensor
        def _(pe):
            for n in range(2):
                pe.wait_ge(raw_in[n], 16)
                for c in range(DC):
                    for a in range(DC):
                        last = nc.tensor.transpose(bank(n)[:, c, a * P:(a + 1) * P], raw[n][:, a, c * P:(c + 1) * P],
                                                   ident[:, :])
                last.then_inc(turned, 1)
            pe.wait_ge(ones_set, 2)
            pe.wait_ge(abs_done, 3)
            for c in range(DC):
                nc.tensor.matmul(psum[:, 2 * BANK:2 * BANK + D], ones[:, :], abs0[:, c, :], start=c == 0,
                                 stop=c == DC - 1)
            for n in range(2):
                for c in range(DC):
                    nc.tensor.matmul(psum[:, (3 + n) * BANK:(4 + n) * BANK], ones[:, :],
                                     abs1[:, c, n * BANK:(n + 1) * BANK], start=c == 0, stop=c == DC - 1)
            nc.tensor.matmul(psum[:, 5 * BANK:5 * BANK + 1], ones[:, :], largest[:, :], start=True, stop=True)\
                .then_inc(sums_full, 1)

        @block.scalar
        def _(act):
            act.wait_ge(turned, 2)
            act.activation(abs0[:, :, :], bank(1), ACT.Abs).then_inc(abs_done, 1)
            act.wait_ge(raw_in[3], 16)
            act.activation(abs1[:, :, :], raw[3][:, :, :], ACT.Abs).then_inc(abs_done, 1)
            act.wait_ge(raw_in[2], 16)
            for n, (parts, src, scale) in enumerate(jobs):
                if n == 2:
                    act.wait_ge(scale_ready, 1)
                split(nc, True, parts[0][:, :, :], parts[1][:, :, :], src, scale, hi_done, n + 1, lo_done)

        @block.vector
        def _(dve):
            for n in range(PARTS):
                dve.wait_ge(ctx_in[n], 16 if n < PARTS - 1 else 32)
                if n == PARTS - 1:
                    dve.wait_ge(ones_set, 2)
                end = cut[n + 1] if n < PARTS - 1 else TILES
                last = nc.vector.reduce_max(part_max[:, n:n + 1], rows[:, cut[n]:end, :].rearrange("p t d -> p (t d)"),
                                            AX.X, apply_absolute_value=True)
            last.then_inc(parts_done, 1)
            dve.wait_ge(parts_done, 1)
            nc.vector.reduce_max(largest[:, :], part_max[:, :], AX.X).then_inc(abs_done, 1)
            dve.wait_ge(bias_in, 32)
            nc.vector.reduce_max(bias_max[:, :], bv[:, :], AX.X, apply_absolute_value=True)
            for n in range(2):
                parts, src, scale = jobs[n]
                split(nc, False, parts[0][:, :, :], parts[1][:, :, :], src, scale, hi_done, n + 1, lo_done)
            dve.wait_ge(sums_full, 1)
            step = Steps(dve, step_sem, 0, 8)
            nc.vector.reduce_max(bound[:, 0:1], psum[:, 2 * BANK:2 * BANK + D], AX.X)
            nc.vector.reduce_max(bound[:, 1:2], psum[:, 3 * BANK:5 * BANK], AX.X)
            step(nc.vector.tensor_copy(largest[:, :], psum[:, 5 * BANK:5 * BANK + 1]))
            step(nc.vector.tensor_scalar(bound[:, :], bound[:, :], largest[:, 0:1], TINY, ALU.mult, ALU.max))
            step(nc.vector.tensor_scalar(bound[:, 0:1], bound[:, 0:1], bias_max[:, 0:1], None, ALU.add))
            step(nc.vector.tensor_scalar(v_unit[:, :], bound[:, :], 1.0 / VALUE_TOP, None, ALU.mult))
            nc.vector.tensor_tensor(out_scale[:, :], gates[:, 0:2], v_unit[:, :], ALU.mult)
            step(nc.vector.reciprocal(vscale[:, :], v_unit[:, :]))
            nc.vector.tensor_scalar(bv[:, :], bv[:, :], vscale[:, 0:1], None, ALU.mult).then_inc(scale_ready, 1)
            for n in range(2, 4):
                parts, src, scale = jobs[n]
                split(nc, False, parts[0][:, :, :], parts[1][:, :, :], src, scale, hi_done, n + 1, lo_done)

    GROUPS = (ROWS + BANK - 1) // BANK
    CH = BANK // P
    KB, VB = KV_COLS // P, (KV_COLS + BANK - 1) // BANK
    BANKS = 8
    rows = [sb(f"rows{p}", [P, CH, D]) for p in range(2)]
    rowsT = [pair(f"rowsT{p}", [P, DC, BANK]) for p in range(2)]
    k_out = [sb(f"k_out{p}", [P, KB, BANK]) for p in range(2)]
    v_out = [sb(f"v_out{p}", [P, CH, 2, KV_COLS], F16) for p in range(2)]
    v_sum = sb("v_sum", [P, D])
    work = [psum[:, s * BANK:(s + 1) * BANK] for s in range(BANKS)]
    work_full = [sem(f"work_full{s}") for s in range(BANKS)]
    rows_in = [sem(f"rows_in{p}") for p in range(2)]
    stored = [sem(f"stored{p}") for p in range(2)]
    rowsT_hi, rowsT_ready, k_ready, v_sum_ready, v_hi, v_ready = (
        sem("rowsT_hi"), sem("rowsT_ready"), sem("k_ready"), sem("v_sum_ready"), sem("v_hi"), sem("v_ready"))

    def count(g):
        return min(BANK, ROWS - g * BANK) if isinstance(g, int) else BANK

    def chunks(g):
        return [min(P, count(g) - c * P) for c in range((count(g) + P - 1) // P)]

    def value_cols(n):
        return slice(0, D) if n == 0 else slice(D + (n - 1) * BANK, D + n * BANK)

    def uses(g):
        turn = [("rowsT", c) for c in range(DC)] if g + 1 < GROUPS else []
        if g < 0:
            return turn
        return [("k", b) for b in range(KB)] + turn + [("v", c, n) for c in range(len(chunks(g))) for n in range(VB)]

    ring = Ring(uses, BANKS, -1, GROUPS, 2)

    def freed(g, use):
        if use[0] == "rowsT":
            return rowsT_ready, (g + 1) * DC + use[1] + 1
        if use[0] == "k":
            return k_ready, g * KB + use[1] + 1
        if use[2] == 0:
            return v_sum_ready, g * CH + use[1] + 1
        return v_ready, (g * CH + use[1]) * VB + use[2]

    def groups(eng, body):
        for g in range(2):
            body(g, g, 0)
        with eng.Fori(1, GROUPS // 2 - 2) as j:
            for p in range(2):
                body(j * 2 + p, p, j)
        for g in range(GROUPS - 4, GROUPS):
            body(g, g % 2, g // 2)

    block = ctx.enter_context(nc.Block())

    @block.sync
    def _(sp):
        def load_rows(g, p):
            n = count(g)
            need(sp, rowsT_ready, (g - 1) * DC)
            span = slice(g * BANK, g * BANK + n // P * P) if isinstance(g, int) else bass.ds(g * BANK, BANK)
            sp.dma_start(rows[p][:, 0:n // P, :], context[span].rearrange("(c p) d -> p c d", p=P))\
                .then_inc(rows_in[p], 16)
            if n % P:
                sp.dma_start(rows[p][0:n % P, n // P, :], context[ROWS - n % P:ROWS]).then_inc(rows_in[p], 16)

        def body(g, p, j):
            at = g * BANK
            n, full = count(g), count(g) // P
            if not isinstance(g, int) or g + 2 < GROUPS:
                load_rows(g + 2, p)
            need(sp, k_ready, (g + 1) * KB)
            span = slice(at, at + n) if isinstance(g, int) else bass.ds(at, n)
            sp.dma_start(kt.rearrange("b p k -> p b k")[:, :, span], k_out[p][:, :, 0:n]).then_inc(stored[p], 16)
            need(sp, v_ready, g * CH * VB + len(chunks(g)) * VB)
            span = slice(at, at + full * P) if isinstance(g, int) else bass.ds(at, full * P)
            sp.dma_start(v[span].rearrange("(c p) k d -> p c k d", p=P), v_out[p][:, 0:full, :, :])\
                .then_inc(stored[p], 16)
            if n % P:
                sp.dma_start(v[at + full * P:at + n], v_out[p][0:n % P, full, :, :]).then_inc(stored[p], 16)

        for g in range(2):
            load_rows(g, g)
        groups(sp, body)
        sp.wait_ge(stored[0], 32 * ((GROUPS + 1) // 2))
        sp.wait_ge(stored[1], 32 * (GROUPS // 2) + (16 if ROWS % P else 0))

    @block.tensor
    def _(pe):
        def bank_for(g, use):
            before = ring.before(g, use)
            if before is not None:
                need(pe, *freed(*before))
            return work[ring.fill(g, use)[0]]

        def filled(ins, g, use):
            ins.then_inc(work_full[ring.fill(g, use)[0]], 1)

        def turn(g, p, before):
            need(pe, rows_in[p], (before + 1) * 16 + (16 if count(g + 1) % P else 0))
            for c in range(DC):
                bank = bank_for(g, ("rowsT", c))
                for a, n in enumerate(chunks(g + 1)):
                    last = nc.tensor.transpose(bank[:, a * P:a * P + n], rows[p][0:n, a, c * P:(c + 1) * P],
                                               ident[0:n, 0:n])
                filled(last, g, ("rowsT", c))

        def body(g, p, j):
            need(pe, rowsT_ready, (g + 1) * DC)
            n = count(g)
            for b in range(KB):
                w, at = (wk, b * P) if b < DC else (wk1, (b - DC) * P)
                bank = bank_for(g, ("k", b))
                for c in range(DC):
                    last = matmul3(nc, bank[:, 0:n], [x[:, c, at:at + P] for x in w],
                                   [x[:, c, 0:n] for x in rowsT[p]], c == 0, c == DC - 1)
                filled(last, g, ("k", b))
            if not isinstance(g, int) or g + 1 < GROUPS:
                turn(g, 1 - p, j + p)
            for a, m in enumerate(chunks(g)):
                for k in range(VB):
                    w, cols = (wv, slice(0, D)) if k == 0 else (wv1, slice((k - 1) * BANK, k * BANK))
                    bank = bank_for(g, ("v", a, k))
                    for c in range(DC):
                        last = matmul3(nc, bank[0:m, 0:cols.stop - cols.start],
                                       [x[:, c, a * P:a * P + m] for x in rowsT[p]], [x[:, c, cols] for x in w],
                                       c == 0, c == DC - 1)
                    filled(last, g, ("v", a, k))

        turn(-1, 0, 0)
        groups(pe, body)

    @block.scalar
    def _(act):
        def full(g, use):
            s, k = ring.fill(g, use)
            need(act, work_full[s], k)
            return work[s]

        def turn(g, p):
            for c in range(DC):
                n = count(g + 1)
                act.activation(rowsT[p][0][:, c, 0:n], full(g, ("rowsT", c))[:, 0:n], ACT.Copy).then_inc(rowsT_hi, 1)

        def body(g, p, j):
            n = count(g)
            need(act, stored[p], j * 32)
            for b in range(KB):
                bank = full(g, ("k", b))[:, 0:n]
                if b < DC:
                    last = act.activation(k_out[p][:, b, 0:n], bank, ACT.Identity, bias=bk[:, b:b + 1])
                else:
                    last = act.activation(k_out[p][:, b, 0:n], bank, ACT.Copy)
                last.then_inc(k_ready, 1)
            if not isinstance(g, int) or g + 1 < GROUPS:
                turn(g, 1 - p)
            for a, m in enumerate(chunks(g)):
                for k in (1, 2, 0):
                    cols = value_cols(k)
                    if k == 0:
                        need(act, v_sum_ready, g * CH + a + 1)
                        src = v_sum[0:m, :]
                    else:
                        src = full(g, ("v", a, k))[0:m, :]
                    act.activation(v_out[p][0:m, a, 0, cols], src, ACT.Copy).then_inc(v_hi, 1)

        turn(-1, 0)
        groups(act, body)

    @block.vector
    def _(dve):
        def full(g, use):
            s, k = ring.fill(g, use)
            need(dve, work_full[s], k)
            return work[s]

        def turn(g, p):
            for c in range(DC):
                n = count(g + 1)
                bank = full(g, ("rowsT", c))
                need(dve, rowsT_hi, (g + 1) * DC + c + 1)
                nc.vector.tensor_tensor(rowsT[p][1][:, c, 0:n], bank[:, 0:n], plain(rowsT[p][0][:, c, 0:n]),
                                        ALU.subtract).then_inc(rowsT_ready, 1)

        def body(g, p, j):
            if not isinstance(g, int) or g + 1 < GROUPS:
                turn(g, 1 - p)
            need(dve, stored[p], j * 32)
            for a, m in enumerate(chunks(g)):
                at = g * CH + a
                need(dve, v_ready, at * VB)
                nc.vector.tensor_tensor(v_sum[0:m, :], full(g, ("v", a, 0))[0:m, 0:D], bv[0:m, :], ALU.add)\
                    .then_inc(v_sum_ready, 1)
                for step, k in enumerate((1, 2, 0)):
                    cols = value_cols(k)
                    src = v_sum[0:m, :] if k == 0 else full(g, ("v", a, k))[0:m, :]
                    need(dve, v_hi, at * VB + step + 1)
                    if k == 0:
                        need(dve, v_sum_ready, at + 1)
                    nc.vector.tensor_tensor(v_out[p][0:m, a, 1, cols], src, v_out[p][0:m, a, 0, cols], ALU.subtract)\
                        .then_inc(v_ready, 1)

        turn(-1, 0)
        groups(dve, body)


def layer0_weights(nc, ctx, psum, const, w_q, b_q, w_o, b_o):
    sb = lambda n, s, d=FP32: ctx.enter_context(nc.sbuf_tensor(f"w0_{n}", s, d))
    sem = lambda n: nc.alloc_semaphore(f"w0_{n}")
    wT = [(sb(f"{n}T_hi", [P, DC, D], F32R), sb(f"{n}T_lo", [P, DC, D], F32R)) for n in "qo"]
    bq, bo = sb("bq", [P, DC]), sb("bo", [P, D])
    raw_in = [sem(f"raw_in{n}") for n in range(2)]
    bias_in, turned, hi_done, lo_done = sem("bias_in"), sem("turned"), sem("hi_done"), sem("lo_done")
    gate = const["gates"][:, 0:1]
    q_scale = float(D // H) ** -0.5
    scales = [1.0, const["out_scale"][:, 0:1]]
    with ExitStack() as inner:
        raw = [inner.enter_context(nc.sbuf_tensor(f"w0_raw{n}", [P, DC, D], FP32)) for n in range(2)]
        block = inner.enter_context(nc.Block())
        bank = lambda n: psum[:, n * BANK:(n + 1) * BANK].rearrange("p (c o) -> p c o", c=DC)

        @block.sync
        def _(sp):
            for n, w in enumerate((w_q, w_o)):
                sp.dma_start(raw[n][:, :, :], w.rearrange("(a p) d -> p a d", p=P)).then_inc(raw_in[n], 16)
            with nc.allow_non_contiguous_dma("biases, one value per partition"):
                sp.dma_start(bq[:, :], b_q.rearrange("(c p) -> p c", p=P)).then_inc(bias_in, 16)
            sp.dma_start(bo[:, :], row(b_o, P, D)).then_inc(bias_in, 16)

        @block.tensor
        def _(pe):
            for n in range(2):
                pe.wait_ge(raw_in[n], 16)
                for c in range(DC):
                    for a in range(DC):
                        last = nc.tensor.transpose(bank(n)[:, c, a * P:(a + 1) * P], raw[n][:, a, c * P:(c + 1) * P],
                                                   const["ident"][:, :])
                last.then_inc(turned, 1)

        @block.scalar
        def _(act):
            for n in range(2):
                act.wait_ge(turned, n + 1)
                split(nc, True, wT[n][0][:, :, :], wT[n][1][:, :, :], bank(n), scales[n], hi_done, n + 1, lo_done)
            act.wait_ge(bias_in, 32)
            act.activation(bq[:, :], bq[:, :], ACT.Copy, scale=q_scale)

        @block.vector
        def _(dve):
            for n in range(2):
                split(nc, False, wT[n][0][:, :, :], wT[n][1][:, :, :], bank(n), scales[n], hi_done, n + 1, lo_done)
            dve.wait_ge(bias_in, 32)
            nc.vector.tensor_scalar(bo[:, :], bo[:, :], gate, None, ALU.mult)
    return (*wT, q_scale, bq, bo)


def layer1_weights(nc, ctx, psum, const, w_q, w_o, protos, low_b, low_a, low_bias, temp, bias0):
    sb = lambda n, s, d=FP32: ctx.enter_context(nc.sbuf_tensor(f"w1_{n}", s, d))
    sem = lambda n: nc.alloc_semaphore(f"w1_{n}")
    pair = lambda n, s: (sb(n + "_hi", s, F32R), sb(n + "_lo", s, F32R))
    W = H * 64
    wq, wo = pair("q", [P, DC, W]), pair("o", [P, W // P, D])
    HALF = LOW // 2
    downT, upT = pair("downT", [P, DC, 2, HALF + NPROTO]), pair("upT", [P, LC, D])
    low_bias_sb, proto_sq = sb("low_bias", [P, D]), sb("proto_sq", [P, NPROTO])
    mit, bias0_row = sb("minus_inv_temp", [P, 1]), sb("bias0", [P, D])
    gates = const["gates"]
    raw_in = [sem(f"raw_in{n}") for n in range(5)]
    small_in, bias_zero, turned, hi_done, lo_done, sq_done, sq_full, step_sem, ones_set = (
        sem("small_in"), sem("bias_zero"), sem("turned"), sem("hi_done"), sem("lo_done"), sem("sq_done"),
        sem("sq_full"), sem("step"), sem("ones_set"))
    with ExitStack() as inner:
        tmp = lambda n, s: inner.enter_context(nc.sbuf_tensor(f"w1_{n}", s, FP32))
        raw = [tmp("raw0", [P, DC, W]), tmp("raw1", [P, W // P, D])]
        raw_p, raw_b, raw_a = tmp("raw_p", [NPROTO, D]), tmp("raw_b", [P, LC, D]), tmp("raw_a", [P, DC, LOW])
        sq, ones, neg = tmp("sq", [P, DC, NPROTO]), tmp("ones", [P, P]), tmp("neg", [P, 1])
        block = inner.enter_context(nc.Block())
        ident = const["ident"]
        cols = lambda n, c, k=1: psum[:, n * BANK:n * BANK + c * k].rearrange("p (c o) -> p c o", c=c)
        jobs = [(wq, raw[0][:, :, :], 1.0), (wo, raw[1][:, :, :], const["out_scale"][:, 1:2])]
        turned_jobs = [([w[:, :, 0, HALF:] for w in downT], cols(0, DC, NPROTO), 1.0)]
        for c in range(DC):
            turned_jobs.append(([w[:, c, :, 0:HALF] for w in downT], cols(1 + c, 2, HALF), 1.0))
        for c in range(LC // 2):
            turned_jobs.append(((upT[0][:, 2 * c:2 * c + 2, :], upT[1][:, 2 * c:2 * c + 2, :]), cols(3 + c, 2, D),
                                gates[:, 3:4]))

        @block.sync
        def _(sp):
            sp.dma_start(raw_p[:, :], protos).then_inc(raw_in[2], 16)
            sp.dma_start(raw_b[:, :, :], low_b.rearrange("n r d -> (n r) d").rearrange("(c p) d -> p c d", p=P))\
                .then_inc(raw_in[3], 16)
            sp.dma_start(raw[0][:, :, :], w_q.rearrange("(c p) h k -> p c (h k)", p=P)).then_inc(raw_in[0], 16)
            sp.dma_start(raw[1][:, :, :], w_o.rearrange("h k d -> (h k) d").rearrange("(b p) d -> p b d", p=P))\
                .then_inc(raw_in[1], 16)
            sp.dma_start(bias0_row[:, :], row(bias0, P, D)).then_inc(small_in, 16)
            sp.dma_start(mit[:, :], row(temp, P, 1)).then_inc(small_in, 16)
            sp.wait_ge(bias_zero, 1)
            sp.dma_start(low_bias_sb[0:NPROTO, :], low_bias).then_inc(small_in, 16)

        @block.gpsimd
        def _(pool):
            pool.memset(low_bias_sb[:, :], 0.0).then_inc(bias_zero, 1)
            pool.memset(ones[:, :], 1.0).then_inc(ones_set, 1)
            with nc.allow_non_contiguous_dma("second low-rank factors, RANK values at a time"):
                for a in range(DC):
                    pool.dma_start(raw_a[:, a, :].rearrange("p (n r) -> p n r", n=NPROTO),
                                   low_a.rearrange("n (a p) r -> a p n r", p=P)[a]).then_inc(raw_in[4], 16)

        @block.tensor
        def _(pe):
            pe.wait_ge(raw_in[2], 16)
            for c in range(DC):
                last = nc.tensor.transpose(cols(0, DC, NPROTO)[:, c, :], raw_p[:, c * P:(c + 1) * P],
                                           ident[0:NPROTO, 0:NPROTO])
            last.then_inc(turned, 1)
            pe.wait_ge(raw_in[3], 16)
            for c in range(DC):
                for b in range(LC):
                    last = nc.tensor.transpose(psum[:, (1 + c) * BANK + b * P:(1 + c) * BANK + (b + 1) * P],
                                               raw_b[:, b, c * P:(c + 1) * P], ident[:, :])
                last.then_inc(turned, 1)
            pe.wait_ge(raw_in[4], 16 * DC)
            for c in range(LC // 2):
                for b in range(2):
                    for a in range(DC):
                        last = nc.tensor.transpose(cols(3 + c, 2, D)[:, b, a * P:(a + 1) * P],
                                                   raw_a[:, a, (2 * c + b) * P:(2 * c + b + 1) * P], ident[:, :])
                last.then_inc(turned, 1)
            pe.wait_ge(sq_done, 1)
            pe.wait_ge(ones_set, 1)
            for c in range(DC):
                last = nc.tensor.matmul(psum[:, 5 * BANK:5 * BANK + NPROTO], ones[:, :], sq[:, c, :], start=c == 0,
                                        stop=c == DC - 1)
            last.then_inc(sq_full, 1)

        @block.scalar
        def _(act):
            act.wait_ge(turned, 1)
            act.activation(sq[:, :, :], cols(0, DC, NPROTO), ACT.Square).then_inc(sq_done, 1)
            for n, (parts, src, scale) in enumerate(turned_jobs):
                act.wait_ge(turned, n + 1)
                split(nc, True, *parts, src, scale, hi_done, n + 1, lo_done)
            for n, (parts, src, scale) in enumerate(jobs):
                act.wait_ge(raw_in[n], 16)
                split(nc, True, parts[0][:, :, :], parts[1][:, :, :], src, scale, hi_done, 0, lo_done)

        @block.vector
        def _(dve):
            for n, (parts, src, scale) in enumerate(turned_jobs):
                split(nc, False, *parts, src, scale, hi_done, n + 1, lo_done)
            for n, (parts, src, scale) in enumerate(jobs):
                split(nc, False, parts[0][:, :, :], parts[1][:, :, :], src, scale, hi_done,
                      len(turned_jobs) + n + 1, lo_done)
            dve.wait_ge(sq_full, 1)
            nc.vector.tensor_copy(proto_sq[:, :], psum[:, 5 * BANK:5 * BANK + NPROTO])
            dve.wait_ge(small_in, 48)
            nc.vector.tensor_scalar(low_bias_sb[:, :], low_bias_sb[:, :], gates[:, 3:4], None, ALU.mult)
            nc.vector.tensor_scalar(bias0_row[:, :], bias0_row[:, :], gates[:, 2:3], None, ALU.mult)
            step = Steps(dve, step_sem, 0, 4)
            step(nc.vector.tensor_scalar(neg[:, :], mit[:, :], -1.0, None, ALU.mult))
            step(nc.vector.tensor_tensor(mit[:, :], mit[:, :], neg[:, :], ALU.max))
            step(nc.vector.tensor_scalar(mit[:, :], mit[:, :], 0.1, -1.0, ALU.max, ALU.mult))
            nc.vector.reciprocal(mit[:, :], mit[:, :])
    ffn = {"down": downT, "up": upT, "bias": low_bias_sb, "proto_sq": proto_sq,
           "minus_inv_temp": mit}
    return wq, wo, bias0_row, ffn


def expert_phase(nc, ctx, psum, const, x1, weights, indices, w1, w2):
    GT = 2 * P
    G = MOE_T // GT
    TG = GT // P
    HN = G * FC
    YN = MOE_TILES
    BANKS = 4
    ident, eps, iota, gates = const["ident"], const["eps"], const["iota"], const["gates"]
    sb = lambda n, s, d=FP32: ctx.enter_context(nc.sbuf_tensor(f"moe_{n}", s, d))
    sem = lambda n: nc.alloc_semaphore(f"moe_{n}")
    pair = lambda n, s: (sb(n + "_hi", s, F32R), sb(n + "_lo", s, F32R))
    xm = sb("x", [P, MOE_TILES, D])
    xn = [sb(f"xn{p}", [P, D]) for p in range(2)]
    xnT = pair("xnT", [P, DC, MOE_T])
    raw1 = [sb(f"raw1_{p}", [P, DC * FF]) for p in range(2)]
    raw2 = [sb(f"raw2_{p}", [P, FC * D]) for p in range(2)]
    w1s = [pair(f"w1_{p}", [P, DC * FF]) for p in range(2)]
    w2s = [pair(f"w2_{p}", [P, FC * D]) for p in range(2)]
    hid = [sb(f"hid{p}", [P, GT]) for p in range(2)]
    hidT = [pair(f"hidT{p}", [P, FC, GT]) for p in range(2)]
    idx, idxf, wts = sb("idx", [P, MOE_TILES, TOPK], I32), sb("idxf", [P, MOE_TILES * TOPK]), sb("wts", [P, MOE_TILES * TOPK])
    choice, comb = sb("choice", [P, MOE_TILES * TOPK, E]), sb("comb", [P, MOE_TILES, E])
    stats, mv = sb("stats", [P, MOE_TILES, 6]), sb("mv", [P, MOE_TILES, 2])
    lnv, rstd, nwt = sb("lnv", [P, MOE_TILES]), sb("rstd", [P, MOE_TILES]), sb("nwt", [P, MOE_TILES])
    hbank = [psum[:, n * BANK:n * BANK + GT] for n in range(BANKS)]
    ybank = [psum[:, (BANKS + n) * BANK:(BANKS + n) * BANK + D] for n in range(BANKS)]
    CH = DC * FF // (HN // 2)

    x_in, route_in, out_done = sem("x_in"), sem("route_in"), sem("out_done")
    w_in = [sem(f"w_in{p}") for p in range(2)]
    chain, ln_stats, ln_log, ln_rough = sem("chain"), sem("ln_stats"), sem("ln_log"), sem("ln_rough")
    xn_ready, xnT_full, xnT_hi, xnT_ready = sem("xn_ready"), sem("xnT_full"), sem("xnT_hi"), sem("xnT_ready")
    wsplit_hi, wsplit = sem("wsplit_hi"), sem("wsplit")
    h_full, gelu_done, hid_hi, hid_ready = sem("h_full"), sem("gelu_done"), sem("hid_hi"), sem("hid_ready")
    y_full, y_added = sem("y_full"), sem("y_added")

    def experts(eng, body):
        with eng.Fori(0, E // 2 - 1) as j:
            for p in range(2):
                body(j * 2 + p, p)
        for p in range(2):
            body(E - 2 + p, p)

    rows = x1.rearrange("b (j p) d -> p (b j) d", p=P)[:, 0:MOE_TILES, :]
    block = ctx.enter_context(nc.Block())

    @block.sync
    def _(sp):
        sp.dma_start(xm[:, :, :], rows).then_inc(x_in, 16)
        sp.dma_start(idx[:, :, :], indices.rearrange("(t p) k -> p t k", p=P)).then_inc(route_in, 16)
        sp.dma_start(wts[:, :].rearrange("p (t k) -> p t k", k=TOPK), weights.rearrange("(t p) k -> p t k", p=P))\
            .then_inc(route_in, 16)
        for e in range(E):
            if e >= 2:
                sp.wait_ge(wsplit, (e - 1) * HN)
            sp.dma_start(raw1[e % 2][:, :].rearrange("p (c f) -> p c f", c=DC),
                         w1[e].rearrange("(c p) f -> p c f", p=P)).then_inc(w_in[e % 2], 16)
            sp.dma_start(raw2[e % 2][:, :].rearrange("p (c d) -> p c d", c=FC),
                         w2[e].rearrange("(c p) d -> p c d", p=P)).then_inc(w_in[e % 2], 16)
        for t in range(MOE_TILES):
            sp.wait_ge(y_added, (E - 1) * YN + t + 1)
            sp.dma_start(rows[:, t, :], xm[:, t, :]).then_inc(out_done, 16)
        sp.wait_ge(out_done, 16 * MOE_TILES)

    @block.scalar
    def _(act):
        load_ln_exp_tables(nc)
        act.wait_ge(ln_stats, 1)
        act.activation(lnv[:, :], mv[:, :, 1], ACT.Ln, bias=eps[:, 0:1]).then_inc(ln_log, 1)
        act.wait_ge(ln_log, 1)
        act.activation(rstd[:, :], lnv[:, :], ACT.Exp, scale=-0.5).then_inc(ln_rough, 1)
        for t in range(MOE_TILES):
            act.wait_ge(xnT_full, t + 1)
            act.activation(xnT[0][:, :, t * P:(t + 1) * P], hbank[t % BANKS].rearrange("p (c s) -> p c s", c=DC),
                           ACT.Copy).then_inc(xnT_hi, 1)

        def body(e, p):
            for n in range(HN):
                g, m, at = n // FC, n % FC, e * HN + n
                act.wait_ge(h_full, at + 1)
                need(act, hid_ready, at - 1)
                act.activation(hid[n % 2][:, :], hbank[n % BANKS], ACT.Gelu).then_inc(gelu_done, 1)
                act.wait_ge(gelu_done, at + 1)
                act.activation(hidT[g % 2][0][:, m, :], hid[n % 2][:, :], ACT.Copy).then_inc(hid_hi, 1)

        def first(e, p):
            body(e, p)

        for p in range(2):
            first(p, p)
        with act.Fori(1, E // 2) as j:
            for p in range(2):
                body(j * 2 + p, p)

    @block.tensor
    def _(pe):
        for t in range(MOE_TILES):
            pe.wait_ge(xn_ready, t + 1)
            if t >= BANKS:
                pe.wait_ge(xnT_ready, t - BANKS + 1)
            for c in range(DC):
                last = nc.tensor.transpose(hbank[t % BANKS][:, c * P:(c + 1) * P], xn[t % 2][:, c * P:(c + 1) * P],
                                           ident[:, :])
            last.then_inc(xnT_full, 1)
        pe.wait_ge(xnT_ready, MOE_TILES)

        def hidden(e, p, g):
            for m in range(FC):
                n = g * FC + m
                need(pe, gelu_done, e * HN + n + 1 - BANKS)
                for c in range(DC):
                    at = c * FF + m * P
                    last = matmul3(nc, hbank[n % BANKS], [w[:, at:at + P] for w in w1s[p]],
                                   [a[:, c, g * GT:(g + 1) * GT] for a in xnT], c == 0, c == DC - 1)
                last.then_inc(h_full, 1)

        def outputs(e, p, g):
            need(pe, hid_ready, e * HN + (g + 1) * FC)
            for a in range(TG):
                n = g * TG + a
                need(pe, y_added, e * YN + n + 1 - BANKS)
                for m in range(FC):
                    last = matmul3(nc, ybank[n % BANKS], [x[:, m, a * P:(a + 1) * P] for x in hidT[g % 2]],
                                   [w[:, m * D:(m + 1) * D] for w in w2s[p]], m == 0, m == FC - 1)
                last.then_inc(y_full, 1)

        def body(e, p):
            need(pe, wsplit, (e + 1) * HN)
            for g in range(G):
                hidden(e, p, g)
                if g > 0:
                    outputs(e, p, g - 1)
            outputs(e, p, G - 1)

        for p in range(2):
            body(p, p)
        with pe.Fori(1, E // 2) as j:
            for p in range(2):
                body(j * 2 + p, p)

    @block.vector
    def _(dve):
        dve.wait_ge(x_in, 16)
        step = Steps(dve, chain, 0, 10)
        for t in range(MOE_TILES):
            last = nc.vector.bn_stats(stats[:, t, :], xm[:, t, :])
        step(last)
        for t in range(MOE_TILES):
            last = nc.vector.bn_aggr(mv[:, t, :], stats[:, t, :])
        last.then_inc(ln_stats, 1)
        dve.wait_ge(route_in, 32)
        step(nc.vector.tensor_copy(idxf[:, :], idx[:, :, :].rearrange("p t k -> p (t k)")))
        step(nc.vector.tensor_scalar(wts[:, :], wts[:, :], gates[:, 2:3], None, ALU.mult))
        n = MOE_TILES * TOPK
        step(nc.vector.tensor_tensor(choice[:, :, :], idxf[:, :].unsqueeze(2).broadcast_to([P, n, E]),
                                     iota[:, 0:E].unsqueeze(1).broadcast_to([P, n, E]), ALU.is_equal))
        step(nc.vector.tensor_tensor(choice[:, :, :], choice[:, :, :], wts[:, :].unsqueeze(2).broadcast_to([P, n, E]),
                                     ALU.mult))
        both = choice[:, :, :].rearrange("p (t k) e -> p t k e", k=TOPK)
        step(nc.vector.tensor_tensor(comb[:, :, :], both[:, :, 0, :], both[:, :, 1, :], ALU.add))
        dve.wait_ge(ln_stats, 1)
        dve.wait_ge(ln_rough, 1)
        step(nc.vector.tensor_tensor(nwt[:, :], rstd[:, :], rstd[:, :], ALU.mult))
        step(nc.vector.scalar_tensor_tensor(out=nwt[:, :], in0=mv[:, :, 1], scalar=EPS, in1=nwt[:, :], op0=ALU.add,
                                            op1=ALU.mult))
        step(nc.vector.tensor_scalar(nwt[:, :], nwt[:, :], -0.5, 1.5, ALU.mult, ALU.add))
        step(nc.vector.tensor_tensor(rstd[:, :], rstd[:, :], nwt[:, :], ALU.mult))

        def normed_lo(t):
            dve.wait_ge(xnT_hi, t + 1)
            nc.vector.tensor_tensor(xnT[1][:, :, t * P:(t + 1) * P], hbank[t % BANKS].rearrange("p (c s) -> p c s", c=DC),
                                    plain(xnT[0][:, :, t * P:(t + 1) * P]), ALU.subtract).then_inc(xnT_ready, 1)

        for t in range(MOE_TILES):
            if t >= 2:
                normed_lo(t - 2)
            nc.vector.tensor_scalar(xn[t % 2][:, :], xm[:, t, :], mv[:, t, 0:1], rstd[:, t:t + 1], ALU.subtract,
                                    ALU.mult).then_inc(xn_ready, 1)
        for t in range(MOE_TILES - 2, MOE_TILES):
            normed_lo(t)

        def split_weights(e, p, n):
            raw, parts = (raw1[p], w1s[p]) if n < HN // 2 else (raw2[p], w2s[p])
            at = n % (HN // 2) * CH
            cols = slice(at, at + CH)
            nc.vector.tensor_copy(parts[0][:, cols], raw[:, cols]).then_inc(wsplit_hi, 1)
            dve.wait_ge(wsplit_hi, e * HN + n + 1)
            nc.vector.tensor_tensor(parts[1][:, cols], raw[:, cols], plain(parts[0][:, cols]), ALU.subtract)\
                .then_inc(wsplit, 1)

        def add_outputs(e, g):
            for a in range(TG):
                t = g * TG + a
                need(dve, y_full, e * YN + t + 1)
                need(dve, y_added, (e - 1) * YN + t + 1)
                nc.vector.scalar_tensor_tensor(out=xm[:, t, :], in0=ybank[t % BANKS], scalar=comb_at(t, e),
                                               in1=xm[:, t, :], op0=ALU.mult, op1=ALU.add).then_inc(y_added, 1)

        def comb_at(t, e):
            return comb[:, t, bass.ds(e, 1)]

        def body(e, p, ahead):
            if ahead:
                need(dve, y_full, e * YN)
                dve.wait_ge(w_in[1 - p], ((e + 1 - (1 - p)) // 2 + 1) * 32 if isinstance(e, int) else turn[0])
            for n in range(HN):
                g, m = n // FC, n % FC
                dve.wait_ge(hid_hi, e * HN + n + 1)
                nc.vector.tensor_tensor(hidT[g % 2][1][:, m, :], hid[n % 2][:, :], plain(hidT[g % 2][0][:, m, :]),
                                        ALU.subtract).then_inc(hid_ready, 1)
                if ahead:
                    split_weights(e + 1, 1 - p, n)
                if m == FC - 2 and g > 0:
                    add_outputs(e, g - 1)
            add_outputs(e, G - 1)

        turn = [None]
        dve.wait_ge(w_in[0], 32)
        for n in range(HN):
            split_weights(0, 0, n)
        for p in range(2):
            body(p, p, True)
        with dve.Fori(1, E // 2 - 1) as j:
            for p in range(2):
                turn[0] = (j + p) * 32 + 32
                body(j * 2 + p, p, True)
        for p in range(2):
            body(E - 2 + p, p, p == 0)


def flamingo_layers(nc, ins, out):
    x1 = nc.dram_tensor("x1", (NB, SEQ, D), FP32).ap()
    batches = lambda a: a.rearrange("b (j p) d -> b p j d", p=P)
    tiles = lambda a: a.rearrange("b (j p) d -> (b j) p d", p=P)
    kt = nc.dram_tensor("kt", (KV_COLS // P, P, ROWS), FP32).ap()
    v = nc.dram_tensor("v", (ROWS, 2, KV_COLS), F16).ap()
    span = lambda i: slice(i * KEYS, (i + 1) * KEYS) if isinstance(i, int) else bass.ds(i * KEYS, KEYS)
    keys = lambda a, b: lambda i: kt.rearrange("b p k -> p b k")[:, a // P:b // P, span(i)]
    values = lambda a, b: lambda i: v[span(i), :, a:b]
    with ExitStack() as ctx:
        psum = ctx.enter_context(nc.psum_tensor("banks", [P, 8 * BANK], FP32))[:, :]
        const = constants(nc, ctx, ins["g_xattn"], ins["g_ffn"])
        with nc.cleanup_on_exit(), ExitStack() as layer:
            keys_values_phase(nc, layer, psum, const, ins["ctx_1024"].rearrange("b k d -> (b k) d"),
                              *(ins[f"L0_xattn_{k}_{n}"] for n in "kv" for k in "wb"), ins["L1_xattn_Wk"],
                              ins["L1_xattn_Wv"], kt, v)
        with nc.cleanup_on_exit(), ExitStack() as layer:
            wq, wo, q_scale, bq, bo = layer0_weights(nc, layer, psum, const,
                                                     *(ins[f"L0_xattn_{k}_{n}"] for n in "qo" for k in "wb"))
            attention_phase(nc, layer, psum, const, "a0", batches(ins["x"]), tiles(x1), keys(0, D), values(0, D),
                            D // H, wq, wo, q_scale, bq, bo, False, None)
        with nc.cleanup_on_exit(), ExitStack() as layer:
            expert_phase(nc, layer, psum, const, x1, ins["L0_ffn_expert_weights"], ins["L0_ffn_expert_indices"],
                         ins["L0_ffn_w1"], ins["L0_ffn_w2"])
        with nc.cleanup_on_exit(), ExitStack() as layer:
            wq, wo, bias0, ffn = layer1_weights(
                nc, layer, psum, const, *(ins[f"L1_xattn_W{n}"] for n in "qo"), ins["L1_ffn_prototypes"],
                ins["L1_ffn_B"], ins["L1_ffn_A"], ins["L1_ffn_bias"], ins["L1_ffn_temp"], ins["L0_ffn_bias"])
            attention_phase(nc, layer, psum, const, "a1", batches(x1), tiles(out), keys(D, KV_COLS),
                            values(D, KV_COLS), 64, wq, wo, 64.0 ** -0.5, None, bias0, True, ffn)


_INS = ["x", "ctx_1024", "g_xattn", "g_ffn", "L0_xattn_w_q", "L0_xattn_b_q", "L0_xattn_w_k", "L0_xattn_b_k",
        "L0_xattn_w_v", "L0_xattn_b_v", "L0_xattn_w_o", "L0_xattn_b_o", "L0_ffn_expert_weights",
        "L0_ffn_expert_indices", "L0_ffn_w1", "L0_ffn_w2", "L0_ffn_bias", "L1_xattn_Wq", "L1_xattn_Wk",
        "L1_xattn_Wv", "L1_xattn_Wo", "L1_ffn_prototypes", "L1_ffn_B", "L1_ffn_A", "L1_ffn_bias", "L1_ffn_temp"]


def kernel(**inputs):
    import numpy as _np
    import concourse.bacc as _bacc
    from concourse import mybir as _mybir
    from concourse.bass_utils import run_bass_kernel_spmd as _run

    nc = _bacc.Bacc("TRN2", target_bir_lowering=False, num_devices=1)
    arrays, ins = {}, {}
    for name in _INS:
        a = _np.ascontiguousarray(inputs[name])
        a = a.reshape(a.shape or (1,))
        arrays[f"in_{name}"] = a
        ins[name] = nc.dram_tensor(f"in_{name}", a.shape, _mybir.dt.from_np(a.dtype), kind="ExternalInput").ap()
    out = nc.dram_tensor("out", (NB, SEQ, D), FP32, kind="ExternalOutput").ap()
    flamingo_layers(nc, ins, out)
    r = _run(nc, [arrays], core_ids=[0])
    return r.results[0]["out"]
```
